# Optimizing a Trainium2 kernel written in Bass

```python
import numpy as np
import jax
import jax.numpy as jnp

def _softmax(x, axis=-1):
    return jax.nn.softmax(x, axis=axis)

def _gelu(x):
    return jax.nn.gelu(x, approximate=True)

def _silu(x):
    return jax.nn.silu(x)

def _sigmoid(x):
    return jax.nn.sigmoid(x)

def _layernorm(x, axis=-1, eps=1e-05):
    m = jnp.mean(x, axis=axis, keepdims=True)
    v = jnp.var(x, axis=axis, keepdims=True)
    return (x - m) / jnp.sqrt(v + eps)

def _scatter_add(tgt, idx, src, axis=0):
    return tgt.at[idx].add(src)

def _segment_sum(src, seg, n):
    return jax.ops.segment_sum(src, seg, n)
kernel_name = 'mk_flamingo_gated_d1_seqx_r8_8f7444'

def setup_inputs(seed: int=0):
    np.random.seed(seed)
    _w = jnp.asarray

    def _rec_inputs():
        import jax
        import jax.numpy as jnp
        _rk = jax.random.key(seed)
        x = -0.0003929 + 0.9999 * jax.random.normal(jax.random.fold_in(_rk, 1), (4, 256, 512), jnp.float32)
        _lenS = 256 - jax.random.randint(jax.random.fold_in(_rk, 7), (4,), 0, max(1, 256 // 4) + 1, jnp.int32)
        _lenS2 = 64 - jax.random.randint(jax.random.fold_in(_rk, 8), (4,), 0, max(1, 64 // 4) + 1, jnp.int32)
        _ctx_4096P = jax.random.normal(jax.random.fold_in(_rk, 11), (4, 16, 512), jnp.float32)
        _ctx_4096c = jax.random.dirichlet(jax.random.fold_in(_rk, 511), 0.3 * jnp.ones((16,), jnp.float32), (4, 64))
        _ctx_4096t = jnp.einsum('bsk,bkd->bsd', _ctx_4096c, _ctx_4096P)
        _ctx_4096t = _ctx_4096t * jax.lax.rsqrt(jnp.mean(jnp.square(_ctx_4096t)) + 1e-12) * 0.953939
        ctx_4096 = 2.81802e-05 + 1.00001 * (_ctx_4096t + 0.3 * jax.random.normal(jax.random.fold_in(_rk, 611), (4, 64, 512), jnp.float32))
        _validS = jnp.arange(256)[None, :] < _lenS[:, None]
        _validS2 = jnp.arange(64)[None, :] < _lenS2[:, None]
        _causal = jnp.tril(jnp.ones((256, 256), dtype=bool))
        mask_SxS2_bk0 = jnp.logical_not(jnp.broadcast_to(_validS2[0:1, :], (256, 64)))
        _g = jax.random.normal(jax.random.fold_in(_rk, 9001), (2, 1), jnp.float32)
        _g = jnp.sign(_g) * jnp.maximum(jnp.abs(_g), 1.0) + (_g == 0) * 1.0
        g_xattn = _g[0]
        g_ffn = _g[1]
        return (x, ctx_4096, mask_SxS2_bk0, g_xattn, g_ffn)
    x, ctx_4096, mask_SxS2_bk0, g_xattn, g_ffn = _rec_inputs()

    def _L0_xattn_setup():
        import jax, jax.numpy as jnp
        import numpy as np
        N_HEAD = 32
        D_MODEL = 512
        N_KV_GROUPS = 8
        D_HEAD = D_MODEL // N_HEAD
        H_PER_G = N_HEAD // N_KV_GROUPS
        KV_DIM = N_KV_GROUPS * D_HEAD
        B, S = (2, 256)
        key = jax.random.key(seed)
        ks = jax.random.split(key, 8)
        q = jax.random.normal(ks[0], (B, S, D_MODEL), dtype=jnp.float32)
        k = jax.random.normal(ks[1], (B, S, D_MODEL), dtype=jnp.float32)
        v = jax.random.normal(ks[2], (B, S, D_MODEL), dtype=jnp.float32)
        mask = jnp.tril(jnp.ones((S, S), dtype=bool))
        w_q = jax.random.uniform(ks[3], (D_MODEL, D_MODEL), dtype=jnp.float32) * 0.02
        w_k = jax.random.uniform(ks[4], (KV_DIM, D_MODEL), dtype=jnp.float32) * 0.02
        w_v = jax.random.uniform(ks[5], (KV_DIM, D_MODEL), dtype=jnp.float32) * 0.02
        w_out = jax.random.uniform(ks[6], (D_MODEL, D_MODEL), dtype=jnp.float32) * 0.02
        return {'q': q, 'k': k, 'v': v, 'w_q': w_q, 'w_k': w_k, 'w_v': w_v, 'w_out': w_out, 'mask': mask}
    _L0_xattn_all = _L0_xattn_setup()
    _L0_xattn_in = {k: v for k, v in _L0_xattn_all.items() if k in ('w_q', 'w_k', 'w_v', 'w_out')}
    del _L0_xattn_all

    def _L0_ffn_setup():
        import jax, jax.numpy as jnp
        import numpy as np
        IN_F = 512
        OUT_F = 512
        RANK = 8
        NUM_EXPERTS = 64
        TOP_K = 16
        ROUTER_DIM = 16
        ALPHA = 32
        SCALING = ALPHA / TOP_K
        BOTTLENECK = NUM_EXPERTS * RANK
        key = jax.random.key(seed)
        ks = jax.random.split(key, 5)
        x = jax.random.normal(ks[0], (4, 512, IN_F), dtype=jnp.float32)
        bound_a = float(np.sqrt(6.0 / IN_F))
        A_w = jax.random.uniform(ks[1], (BOTTLENECK, IN_F), jnp.float32, -bound_a, bound_a)
        B_w = jax.random.normal(ks[2], (OUT_F, BOTTLENECK), dtype=jnp.float32) * 0.02
        Wq_w = jax.random.normal(ks[3], (ROUTER_DIM, IN_F), dtype=jnp.float32) * 0.02
        keys = jax.random.normal(ks[4], (NUM_EXPERTS, ROUTER_DIM), dtype=jnp.float32) * 0.01
        return {'x': x, 'A_w': A_w, 'B_w': B_w, 'Wq_w': Wq_w, 'keys': keys}
    _L0_ffn_all = _L0_ffn_setup()
    _L0_ffn_in = {k: v for k, v in _L0_ffn_all.items() if k in ('A_w', 'B_w', 'Wq_w', 'keys')}
    del _L0_ffn_all
    return {'x': x, 'ctx_4096': ctx_4096, 'mask_SxS2_bk0': mask_SxS2_bk0, 'g_xattn': g_xattn, 'g_ffn': g_ffn, 'L0_xattn_w_q': _L0_xattn_in['w_q'], 'L0_xattn_w_k': _L0_xattn_in['w_k'], 'L0_xattn_w_v': _L0_xattn_in['w_v'], 'L0_xattn_w_out': _L0_xattn_in['w_out'], 'L0_ffn_A_w': _L0_ffn_in['A_w'], 'L0_ffn_B_w': _L0_ffn_in['B_w'], 'L0_ffn_Wq_w': _L0_ffn_in['Wq_w'], 'L0_ffn_keys': _L0_ffn_in['keys']}

def reference(x, ctx_4096, mask_SxS2_bk0, g_xattn, g_ffn, L0_xattn_w_q, L0_xattn_w_k, L0_xattn_w_v, L0_xattn_w_out, L0_ffn_A_w, L0_ffn_B_w, L0_ffn_Wq_w, L0_ffn_keys):
    import jax
    import jax.numpy as jnp

    def _L0_xattn_ref(q, k, v, w_q, w_k, w_v, w_out, mask):
        import jax, jax.numpy as jnp
        import numpy as np
        N_HEAD = 32
        D_MODEL = 512
        N_KV_GROUPS = 8
        D_HEAD = D_MODEL // N_HEAD
        H_PER_G = N_HEAD // N_KV_GROUPS
        KV_DIM = N_KV_GROUPS * D_HEAD
        B, S = (2, 256)
        b, n, _ = q.shape
        s = k.shape[1]
        query = q @ w_q.T
        key = k @ w_k.T
        value = v @ w_v.T
        query = query.reshape(b, n, N_HEAD, D_HEAD).transpose(0, 2, 1, 3)
        query = query.reshape(b, N_KV_GROUPS, H_PER_G, n, D_HEAD)
        key = key.reshape(b, s, N_KV_GROUPS, D_HEAD).transpose(0, 2, 1, 3)
        value = value.reshape(b, s, N_KV_GROUPS, D_HEAD).transpose(0, 2, 1, 3)
        scores = jnp.einsum('bghnd,bgsd->bghns', query, key) / D_HEAD ** 0.5
        scores = jnp.where(mask, scores, jnp.finfo(scores.dtype).min)
        attention = jax.nn.softmax(scores, axis=-1)
        out = jnp.einsum('bghns,bgsd->bghnd', attention, value)
        out = out.transpose(0, 3, 1, 2, 4).reshape(b, n, D_MODEL)
        return out @ w_out.T

    def _L0_ffn_ref(x, A_w, B_w, Wq_w, keys):
        import jax, jax.numpy as jnp
        import numpy as np
        IN_F = 512
        OUT_F = 512
        RANK = 8
        NUM_EXPERTS = 64
        TOP_K = 16
        ROUTER_DIM = 16
        ALPHA = 32
        SCALING = ALPHA / TOP_K
        BOTTLENECK = NUM_EXPERTS * RANK
        q = jnp.einsum('bsd,rd->bsr', x, Wq_w)
        scores = jnp.einsum('bsr,er->bse', q, keys)
        top_vals, top_idx = jax.lax.top_k(scores, TOP_K)
        top_w = jax.nn.softmax(top_vals, axis=-1)
        gate = jnp.sum(jax.nn.one_hot(top_idx, NUM_EXPERTS, dtype=top_w.dtype) * top_w[..., None], axis=-2)
        z = jnp.einsum('bsd,nd->bsn', x, A_w)
        z = z.reshape(*z.shape[:-1], NUM_EXPERTS, RANK)
        z_gated = (z * gate[..., None]).reshape(*z.shape[:-2], BOTTLENECK)
        out = jnp.einsum('bsn,on->bso', z_gated, B_w) * SCALING
        return out
    x = x + jnp.tanh(g_xattn[0]) * _L0_xattn_ref(_layernorm(x, axis=-1), ctx_4096, ctx_4096, L0_xattn_w_q, L0_xattn_w_k, L0_xattn_w_v, L0_xattn_w_out, mask_SxS2_bk0)
    x = x + jnp.tanh(g_ffn[0]) * _L0_ffn_ref(_layernorm(x, axis=-1), L0_ffn_A_w, L0_ffn_B_w, L0_ffn_Wq_w, L0_ffn_keys)
    return x

_drawn_inputs = setup_inputs


def setup_inputs(seed=0):
    import zlib

    import numpy as np

    out = dict(_drawn_inputs(seed))
    spreads = {}
    factors = {'L0_xattn_w_q': 8.0,
     'L0_xattn_w_k': 8.0,
     'L0_xattn_w_out': 4.212,
     'L0_ffn_A_w': 3.183,
     'L0_ffn_B_w': 2.908,
     'L0_ffn_Wq_w': 3.426,
     'L0_ffn_keys': 3.452}
    for name, (base, spread) in spreads.items():
        noise = np.random.default_rng([zlib.crc32(name.encode()), seed]).standard_normal(out[name].shape)
        drawn = base * np.exp(spread * noise) if base else spread * noise
        out[name] = jnp.asarray(drawn.astype(out[name].dtype))
    for name, factor in factors.items():
        out[name] = (out[name] * factor).astype(out[name].dtype)
    return out
```

```python
import concourse.bass as bass
from concourse import mybir
from contextlib import ExitStack


def gated_cross_attention_kernel(nc, x_in, ctxT_in, mask_in, g_attn_in, g_ffn_in,
                                 wqT_in, wkT_in, wvT_in, woT_in, aT_in, bT_in, wr_in, keysT_in,
                                 out):
    f32 = mybir.dt.float32
    f32r = mybir.dt.float32r
    bf16 = mybir.dt.bfloat16
    ALU = mybir.AluOpType
    ACT = mybir.ActivationFunctionType
    AX = mybir.AxisListType

    P = 128
    B, S, D = x_in.shape
    CT = ctxT_in.shape[2]
    KV = wkT_in.shape[1]
    E = keysT_in.shape[1]
    R = wr_in.shape[0]
    H, DH = 32, 16
    G = KV // DH
    HG = H // G
    RANK = D // E
    TB = S // P
    NT = B * TB
    DC = D // P
    GW = HG * CT
    PAIRS = H // 2
    SB = 4
    ZA = 288
    ZB = D - ZA
    EA = ZA // RANK
    EPS = 1e-5
    SCALE = DH ** -0.5
    SCALING = 32 / 16
    BIG = 3.3895313892515355e38
    TAKEN = -3.0e38

    ctx = ExitStack()
    with ctx:
        def sb(name, shape, dt=f32):
            return ctx.enter_context(nc.sbuf_tensor(name, shape, dt))

        def pb(name):
            return ctx.enter_context(nc.psum_tensor(name, [P, 512], f32))

        def sem(name):
            return ctx.enter_context(nc.semaphore(name))

        x = sb("x", [P, NT, D])
        wq = sb("wq", [P, DC, D])
        wo = sb("wo", [P, DC, D])
        aw = sb("aw", [P, DC, D + E])
        bw = sb("bw", [P, DC, D])
        wq_hi, wq_lo = sb("wq_hi", [P, DC, D], f32r), sb("wq_lo", [P, DC, D], f32r)
        wo_hi, wo_lo = sb("wo_hi", [P, DC, D], f32r), sb("wo_lo", [P, DC, D], f32r)
        aw_hi, aw_lo = sb("aw_hi", [P, DC, D + E], f32r), sb("aw_lo", [P, DC, D + E], f32r)
        bw_hi, bw_lo = sb("bw_hi", [P, DC, D], f32r), sb("bw_lo", [P, DC, D], f32r)
        wk = sb("wk", [P, DC, KV])
        wv = sb("wv", [P, DC, KV])
        ctxT = sb("ctxT", [P, DC, B, CT])
        mask = sb("mask", [P, TB, CT], mask_in.dtype)
        gates = sb("gates", [P, 2])
        wr = sb("wr", [R, D])
        keysT = sb("keysT", [R, E])

        ident = sb("ident", [P, P])
        ident_bf = sb("ident_bf", [P, P], bf16)
        head_of_four = sb("head_of_four", [P, HG])
        half = sb("half", [P, 2])
        neg_half = sb("neg_half", [P, TB])
        mask_add = sb("mask_add", [P, TB, CT], bf16)
        tanh_g = sb("tanh_g", [P, 2])

        wk_heads = sb("wk_heads", [P, DC, D])
        k_hi, k_lo = sb("k_hi", [P, DC, B, CT], f32r), sb("k_lo", [P, DC, B, CT], f32r)
        kb_hi = sb("kb_hi", [P, DC, HG, CT], f32r)
        kb_lo = sb("kb_lo", [P, DC, HG, CT], f32r)
        v = sb("v", [P, B, G, DH])
        vb = sb("vb", [P, G, 2, DH])

        stats = sb("stats", [P, TB, 6])
        mv = sb("mv", [P, TB, 2])
        veps = sb("veps", [P, TB])
        rstd = sb("rstd", [P, TB])
        xn = sb("xn", [P, TB, D])
        xT_hi, xT_lo = sb("xT_hi", [P, DC, S], f32r), sb("xT_lo", [P, DC, S], f32r)
        qT_hi, qT_lo = sb("qT_hi", [P, DC, S], f32r), sb("qT_lo", [P, DC, S], f32r)

        probs = sb("probs", [P, 2, G, GW])
        smax = sb("smax", [P, SB, 2 * HG])
        den = sb("den", [P, SB, 2 * HG])
        rden = sb("rden", [P, SB, 2 * HG])
        rden_wide = sb("rden_wide", [P, H, DH])
        pT = wk_heads[:].rearrange("p c n -> p (c n)").rearrange("p (a n) -> p a n", n=P)
        rdenT, attn, xn2, zg = (wq[:, c, :] for c in range(DC))
        attn_hi, attn_lo = sb("attn_hi", [P, DC, P], f32r), sb("attn_lo", [P, DC, P], f32r)

        stats2 = sb("stats2", [P, 6])
        mv2 = sb("mv2", [P, 2])
        veps2 = sb("veps2", [P, 1])
        rstd2 = sb("rstd2", [P, 1])
        x2T_hi, x2T_lo = sb("x2T_hi", [P, DC, P], f32r), sb("x2T_lo", [P, DC, P], f32r)
        logits = sb("logits", [P, 2, E])
        part = sb("part", [P, E])
        top = sb("top", [P, 2, 8])
        neg_top = sb("neg_top", [P, 1])
        e_exp = sb("e_exp", [P, 2, E])
        gate = sb("gate", [P, E])
        gate_sum = sb("gate_sum", [P, 1])
        gate_scale = sb("gate_scale", [P, 1])
        zgT_hi, zgT_lo = sb("zgT_hi", [P, DC, P], f32r), sb("zgT_lo", [P, DC, P], f32r)

        ps_s = [pb(f"ps_s{i}") for i in range(3)]
        ps_t = [pb(f"ps_t{i}") for i in range(2)]
        ps_m = [pb(f"ps_m{i}") for i in range(3)]
        score_bank = [ps_s[0], ps_s[1], ps_s[2], ps_s[0]]

        q_bank = [ps_m[0], ps_t[1]]

        def bank_probs(t, j):
            g0 = 4 * (j // 2) + j % 2
            return probs[:, t % 2, g0:g0 + 3:2, :]

        x_in_s = [sem(f"x_loaded{b}") for b in range(B)]
        wq_in_s = [sem(f"wq_loaded{c}") for c in range(DC)]
        wo_in_s, aw_in_s, bw_in_s = (sem(n) for n in ("wo_loaded", "aw_loaded", "bw_loaded"))
        ctx_in_s, wk_in_s, wv_in_s, small_in_s = (sem(n) for n in ("ctx_loaded", "wk_loaded", "wv_loaded", "small_loaded"))
        pool_step = sem("pool_step")
        consts = sem("consts_ready")
        tanh_ready = sem("tanh_ready")
        mask_ready = sem("mask_ready")
        wk_heads_ready = sem("wk_heads_ready")
        wq_hi_ready, wq_lo_ready = sem("wq_hi_ready"), sem("wq_lo_ready")
        w_split = sem("w_split")
        aw_hi_ready, aw_ready = sem("aw_hi_ready"), sem("aw_ready")
        k_ready, v_ready, m_ready = sem("k_ready"), sem("v_ready"), sem("m_ready")
        k_hi_done, k_lo_done, v_done, m_hi_done, m_lo_done = (sem(n) for n in ("k_hi_done", "k_lo_done", "v_done", "m_hi_done", "m_lo_done"))
        kb_hi_done, kb_lo_done, vb_done = sem("kb_hi_done"), sem("kb_lo_done"), sem("vb_done")
        dve_step = sem("dve_step")
        var_ready, rstd_ready = sem("var_ready"), sem("rstd_ready")
        xn_ready, xT_ready, xT_hi_done, xT_lo_done = (sem(n) for n in ("xn_ready", "xT_ready", "xT_hi_done", "xT_lo_done"))
        q_ready, q_hi_done, q_lo_done = sem("q_ready"), sem("q_hi_done"), sem("q_lo_done")
        s_ready, sub_done, exp_done = sem("scores_ready"), sem("sub_done"), sem("exp_done")
        rden_done = sem("rden_done")
        pT_ready, pT_done = sem("pT_ready"), sem("pT_done")
        pv_ready, rT_ready, rT_done, attn_done = (sem(n) for n in ("pv_ready", "rdenT_ready", "rdenT_done", "attn_done"))
        attn_hi_done, attn_lo_done = sem("attn_hi_done"), sem("attn_lo_done")
        o_ready, x2_done = sem("o_ready"), sem("x2_done")
        var2_ready, rstd2_ready, xn2_ready = sem("var2_ready"), sem("rstd2_ready"), sem("xn2_ready")
        x2T_ready, x2T_hi_done, x2T_lo_done = sem("x2T_ready"), sem("x2T_hi_done"), sem("x2T_lo_done")
        z_ready, top_done, e_exp_done, zg_done = sem("z_ready"), sem("top_done"), sem("e_exp_done"), sem("zg_done")
        zgT_ready, zgT_hi_done, zgT_lo_done = sem("zgT_ready"), sem("zgT_hi_done"), sem("zgT_lo_done")
        y_ready, y_done, stored = sem("y_ready"), sem("y_done"), sem("stored")

        def chunks(w):
            return w.rearrange("(c p) n -> p c n", p=P)

        def split3(pe, to, lhs_hi, lhs_lo, rhs_hi, rhs_lo, first, last):
            pe.matmul(to, lhs_hi, rhs_hi, start=first, stop=False)
            pe.matmul(to, lhs_hi, rhs_lo, start=False, stop=False)
            return pe.matmul(to, lhs_lo, rhs_hi, start=False, stop=last)

        block = ctx.enter_context(nc.Block())

        @block.sync
        def _(sp):
            xv = x_in.rearrange("b (t p) d -> p (b t) d", p=P)
            ov = out.rearrange("b (t p) d -> p (b t) d", p=P)
            for c in range(TB):
                sp.dma_start(x[:, c:c + 1, :], xv[:, c:c + 1, :]).then_inc(x_in_s[0], 16)
            for c in range(DC):
                sp.dma_start(wq[:, c:c + 1, :], chunks(wqT_in)[:, c:c + 1, :]).then_inc(wq_in_s[c], 16)
            sp.dma_start(wo[:, :, :], chunks(woT_in)).then_inc(wo_in_s, 16)
            sp.dma_start(x[:, 2:4, :], xv[:, 2:4, :]).then_inc(x_in_s[1], 16)
            sp.dma_start(aw[:, :, 0:D], chunks(aT_in)).then_inc(aw_in_s, 16)
            sp.dma_start(bw[:, :, :], chunks(bT_in)).then_inc(bw_in_s, 16)
            for b in range(2, B):
                sp.dma_start(x[:, TB * b:TB * (b + 1), :], xv[:, TB * b:TB * (b + 1), :]).then_inc(x_in_s[b], 16)
            for t in range(NT):
                sp.wait_ge(y_done, t + 1)
                sp.dma_start(ov[:, t:t + 1, :], x[:, t:t + 1, :]).then_inc(stored, 16)
            sp.wait_ge(stored, 16 * NT)

        @block.gpsimd
        def _(pool):
            step = [0]

            def then(ins):
                step[0] += 1
                ins.then_inc(pool_step, 1)
                pool.wait_ge(pool_step, step[0])

            def signal(ins, to, value):
                ins.then_inc(to, 1)
                pool.wait_ge(to, value)

            then(pool.memset(neg_half[:], -0.5))
            then(pool.memset(ident[:], 0.0))
            then(pool.affine_select(out=ident[:], in_=ident[:], compare_op=ALU.not_equal, fill=1.0,
                                    base=0, pattern=[[-1, P]], channel_multiplier=1))
            signal(pool.tensor_copy(ident_bf[:], ident[:]), consts, 1)
            then(pool.memset(half[:], 1.0))
            then(pool.affine_select(out=half[:], in_=half[:], compare_op=ALU.is_ge, fill=0.0,
                                    base=0, pattern=[[-CT, 2]], channel_multiplier=1))
            signal(pool.affine_select(out=half[:], in_=half[:], compare_op=ALU.is_ge, fill=0.0,
                                      base=CT - 1, pattern=[[CT, 2]], channel_multiplier=-1), consts, 2)
            then(pool.memset(head_of_four[:], SCALE))
            for g2 in range(2):
                rows = head_of_four[64 * g2:64 * (g2 + 1), :]
                then(pool.affine_select(out=rows, in_=rows, compare_op=ALU.is_ge, fill=0.0,
                                        base=0, pattern=[[-DH, HG]], channel_multiplier=1))
                signal(pool.affine_select(out=rows, in_=rows, compare_op=ALU.is_ge, fill=0.0,
                                          base=DH - 1, pattern=[[DH, HG]], channel_multiplier=-1), consts, 3 + g2)

            def inv_sqrt(out_, veps_, var):
                then(pool.tensor_scalar(veps_, var, EPS, 0.0, ALU.add, ALU.add))
                return pool.tensor_tensor(out_, veps_, neg_half[:, 0:veps_.shape[1]], ALU.pow)

            def rstd_batch(b):
                pool.wait_ge(var_ready, b + 1)
                signal(inv_sqrt(rstd[:], veps[:], mv[:, :, 1]), rstd_ready, b + 1)

            def split_weight(hi, lo, w, loaded, n):
                pool.wait_ge(loaded, 16)
                for c in range(DC):
                    then(pool.tensor_scalar(hi[:, c, 0:D], w[:, c, 0:D], 1.0, 0.0, ALU.mult, ALU.add))
                    signal(pool.tensor_tensor(lo[:, c, 0:D], w[:, c, 0:D], hi[:, c, 0:D].bitcast(f32),
                                              ALU.subtract), w_split, DC * n + c + 1)

            def key_lows(b):
                if b:
                    pool.wait_ge(s_ready, SB * TB * b)
                for hh in range(HG):
                    signal(pool.tensor_scalar(kb_lo[:, :, hh, :], k_lo[:, :, b, :].bitcast(f32),
                                              head_of_four[:, hh:hh + 1], 0.0, ALU.mult, ALU.add),
                           kb_lo_done, HG * b + hh + 1)

            rstd_batch(0)
            pool.wait_ge(k_lo_done, 1)
            key_lows(0)
            split_weight(wo_hi, wo_lo, wo, wo_in_s, 0)
            split_weight(aw_hi, aw_lo, aw, aw_in_s, 1)
            split_weight(bw_hi, bw_lo, bw, bw_in_s, 2)
            for s in range(NT):
                if s % TB == 0 and s + TB < NT:
                    rstd_batch(s // TB + 1)
                    key_lows(s // TB + 1)
                pool.wait_ge(var2_ready, s + 1)
                signal(inv_sqrt(rstd2[:], veps2[:], mv2[:, 1:2]), rstd2_ready, s + 1)

        @block.scalar
        def _(act):
            for b in range(B):
                act.dma_start(ctxT[:, :, b, :], ctxT_in[b, :, :].rearrange("(c p) s -> p c s", p=P)).then_inc(ctx_in_s, 16)
            act.dma_start(wk[:, :, :], chunks(wkT_in)).then_inc(wk_in_s, 16)
            act.dma_start(wv[:, :, :], chunks(wvT_in)).then_inc(wv_in_s, 16)
            act.dma_start(wr[:, :], wr_in).then_inc(small_in_s, 16)
            act.dma_start(keysT[:, :], keysT_in).then_inc(small_in_s, 16)
            act.dma_start(mask[:, :, :], mask_in.rearrange("(t p) s -> p t s", p=P)).then_inc(small_in_s, 16)
            act.dma_start(gates[:, 0:1], g_attn_in.partition_broadcast(P)).then_inc(small_in_s, 16)
            act.dma_start(gates[:, 1:2], g_ffn_in.partition_broadcast(P)).then_inc(small_in_s, 16)

            def copy_hi(to, src, done):
                act.copy(to, src).then_inc(done, 1)

            def flat(a):
                return a.rearrange("p c n -> p (c n)")

            for c in range(DC):
                act.wait_ge(wq_in_s[c], 16)
                copy_hi(wq_hi[:, c, :], wq[:, c, :], wq_hi_ready)
            act.wait_ge(small_in_s, 80)
            act.activation(tanh_g[:], gates[:], ACT.Tanh).then_inc(tanh_ready, 1)

            def queries_T(b):
                for t in range(TB):
                    act.wait_ge(xT_ready, TB * b + t + 1)
                    copy_hi(xT_hi[:, :, P * t:P * (t + 1)], ps_t[t][:].rearrange("p (c n) -> p c n", c=DC), xT_hi_done)

            def queries(b):
                for j in range(2):
                    act.wait_ge(q_ready, 2 * b + j + 1)
                    copy_hi(qT_hi[:, 2 * j:2 * j + 2, :], q_bank[j][:].rearrange("p (c n) -> p c n", c=2), q_hi_done)

            def exps(t, j):
                act.wait_ge(sub_done, SB * t + j + 1)
                view = bank_probs(t, j)
                act.activation(view, view, ACT.Exp).then_inc(exp_done, 1)

            def probs_T(t, c):
                act.wait_ge(pT_ready, DC * t + c + 1)
                if t:
                    act.wait_ge(pv_ready, t)
                act.copy(pT[:, 4 * c:4 * (c + 1), :].rearrange("p a n -> p (a n)"), ps_t[c % 2][:]).then_inc(pT_done, 1)

            queries_T(0)
            act.wait_ge(k_ready, 1)
            for j in range(2):
                copy_hi(k_hi[:, 2 * j:2 * j + 2, :, :].rearrange("p c b s -> p (c b s)"), ps_s[j][:], k_hi_done)
            queries(0)
            act.wait_ge(m_ready, 1)
            copy_hi(aw_hi[:, :, D:D + E], ps_m[2][:, 0:DC * E].rearrange("p (c e) -> p c e", c=DC), m_hi_done)
            for j in range(SB):
                exps(0, j)
            for s in range(NT + 1):
                if s < NT:
                    for c in range(2):
                        probs_T(s, c)
                    if s + 1 < NT:
                        exps(s + 1, 0)
                    probs_T(s, 2)
                    if s + 1 < NT:
                        exps(s + 1, 1)
                    probs_T(s, 3)
                    act.wait_ge(rT_ready, s + 1)
                    if s:
                        act.wait_ge(attn_done, s)
                    act.copy(rdenT, ps_t[0][:]).then_inc(rT_done, 1)
                    if s + 1 < NT:
                        exps(s + 1, 2)
                    act.wait_ge(attn_done, s + 1)
                    if s:
                        act.wait_ge(o_ready, s)
                    act.copy(flat(attn_hi[:]), attn).then_inc(attn_hi_done, 1)
                    if s + 1 < NT:
                        exps(s + 1, 3)
                if s:
                    act.wait_ge(top_done, s)
                    act.activation(e_exp[:], logits[:], ACT.Exp, bias=neg_top[:]).then_inc(e_exp_done, 1)
                if s % TB == 0 and s + TB < NT:
                    queries_T(s // TB + 1)
                    queries(s // TB + 1)
                if s:
                    act.wait_ge(zgT_ready, s)
                    if s > 1:
                        act.wait_ge(y_ready, s - 1)
                    copy_hi(flat(zgT_hi[:]), ps_t[0][:], zgT_hi_done)
                if s < NT:
                    act.wait_ge(x2T_ready, s + 1)
                    if s:
                        act.wait_ge(z_ready, s)
                    copy_hi(flat(x2T_hi[:]), ps_t[1][:], x2T_hi_done)

        @block.vector
        def _(dve):
            step = [0]

            def then(ins):
                step[0] += 1
                ins.then_inc(dve_step, 1)
                dve.wait_ge(dve_step, step[0])

            def low(to, whole, hi):
                return dve.tensor_tensor(to, whole, hi.bitcast(f32), ALU.subtract)

            def flat(a):
                return a.rearrange("p c n -> p (c n)")

            def norm_batch_stats(b):
                dve.wait_ge(x_in_s[b], 16 * (TB if b == 0 else 1))
                for t in range(TB):
                    then(dve.bn_stats(stats[:, t, :], x[:, TB * b + t, :]))
                    ins = dve.bn_aggr(mv[:, t, :], stats[:, t, :])
                ins.then_inc(var_ready, 1)

            def norm_batch_apply(b):
                dve.wait_ge(rstd_ready, b + 1)
                if b:
                    dve.wait_ge(xT_ready, TB * b)
                for t in range(TB):
                    dve.tensor_scalar(xn[:, t, :], x[:, TB * b + t, :], mv[:, t, 0:1], rstd[:, t:t + 1],
                                      ALU.subtract, ALU.mult).then_inc(xn_ready, 1)

            def queries_T(b):
                for t in range(TB):
                    dve.wait_ge(xT_hi_done, TB * b + t + 1)
                    low(xT_lo[:, :, P * t:P * (t + 1)], ps_t[t][:].rearrange("p (c n) -> p c n", c=DC),
                        xT_hi[:, :, P * t:P * (t + 1)]).then_inc(xT_lo_done, 1)

            def queries(b):
                for j in range(2):
                    dve.wait_ge(q_hi_done, 2 * b + j + 1)
                    low(qT_lo[:, 2 * j:2 * j + 2, :], q_bank[j][:].rearrange("p (c n) -> p c n", c=2),
                        qT_hi[:, 2 * j:2 * j + 2, :]).then_inc(q_lo_done, 1)

            def key_highs(b):
                if b:
                    dve.wait_ge(s_ready, SB * TB * b)
                for hh in range(HG):
                    last = dve.tensor_scalar(kb_hi[:, :, hh, :], k_hi[:, :, b, :].bitcast(f32),
                                             head_of_four[:, hh:hh + 1], None, ALU.mult)
                last.then_inc(kb_hi_done, 1)

            def values(b):
                if b:
                    dve.wait_ge(pv_ready, TB * b)
                for h in range(2):
                    last = dve.tensor_scalar(vb[:, :, h, :], v[:, b, :, :], half[:, h:h + 1], None, ALU.mult)
                last.then_inc(vb_done, 1)

            def softmax_shift(t, j):
                heads = score_bank[j][:].rearrange("p (h s) -> p h s", s=CT)
                dve.wait_ge(s_ready, SB * t + j + 1)
                then(dve.reduce_max(smax[:, j, :], heads, AX.X))
                if t >= 2 and j == 0:
                    dve.wait_ge(pT_ready, DC * (t - 1))
                dve.tensor_tensor(bank_probs(t, j).rearrange("p g (h s) -> p g h s", s=CT),
                                  score_bank[j][:].rearrange("p (g h s) -> p g h s", g=2, s=CT),
                                  smax[:, j, :].rearrange("p (g h) -> p g h", g=2).unsqueeze(3)
                                  .to_broadcast([P, 2, HG, CT]), ALU.subtract).then_inc(sub_done, 1)

            def softmax_sum(t, j):
                dve.wait_ge(exp_done, SB * t + j + 1)
                return dve.reduce_sum(den[:, 2 * (j // 2):2 * (j // 2) + 2, (j % 2) * HG:(j % 2 + 1) * HG],
                                      bank_probs(t, j).rearrange("p g (h s) -> p g h s", s=CT), AX.X)

            def softmax_norm(t):
                then(dve.reciprocal(rden[:], den[:]))
                if t:
                    dve.wait_ge(rT_ready, t)
                dve.tensor_copy(rden_wide[:], rden[:].rearrange("p j h -> p (j h)").unsqueeze(2).to_broadcast([P, H, DH])) \
                    .then_inc(rden_done, 1)

            norm_batch_stats(0)
            dve.wait_ge(wk_in_s, 16)
            for c in range(DC):
                src = wk[:, c, :].rearrange("p (g d) -> p g d", g=G)
                for hh in range(HG):
                    ins = dve.tensor_copy(wk_heads[:, c, :].rearrange("p (g h d) -> p g h d", g=G, h=HG)[:, :, hh, :], src)
            ins.then_inc(wk_heads_ready, 1)
            norm_batch_apply(0)
            for c in range(DC):
                dve.wait_ge(wq_hi_ready, c + 1)
                low(wq_lo[:, c, :], wq[:, c, :], wq_hi[:, c, :]).then_inc(wq_lo_ready, 1)
            queries_T(0)
            for j in range(2):
                dve.wait_ge(k_hi_done, j + 1)
                ins = low(k_lo[:, 2 * j:2 * j + 2, :, :].rearrange("p c b s -> p (c b s)"), ps_s[j][:],
                          k_hi[:, 2 * j:2 * j + 2, :, :].rearrange("p c b s -> p (c b s)"))
            ins.then_inc(k_lo_done, 1)
            dve.wait_ge(small_in_s, 80)
            dve.tensor_scalar(mask_add[:], mask[:], 1.0, BIG, ALU.subtract, ALU.mult).then_inc(mask_ready, 1)
            dve.wait_ge(consts, 4)
            key_highs(0)
            queries(0)
            dve.wait_ge(v_ready, 1)
            then(dve.tensor_copy(v[:].rearrange("p b g d -> p (b g d)"), ps_s[2][:]))
            values(0)
            dve.wait_ge(m_hi_done, 1)
            low(aw_lo[:, :, D:D + E], ps_m[2][:, 0:DC * E].rearrange("p (c e) -> p c e", c=DC),
                aw_hi[:, :, D:D + E]).then_inc(m_lo_done, 1)
            for j in range(SB):
                softmax_shift(0, j)
            for j in range(SB):
                ins = softmax_sum(0, j)
            then(ins)
            softmax_norm(0)

            for s in range(NT + 1):
                more = s + 1 < NT
                if more:
                    for j in range(SB):
                        softmax_shift(s + 1, j)
                if s % TB == 0 and s + TB < NT:
                    b = s // TB + 1
                    key_highs(b)
                    norm_batch_stats(b)
                if s < NT:
                    dve.wait_ge(pv_ready, s + 1)
                    dve.wait_ge(rT_done, s + 1)
                    if s:
                        dve.wait_ge(attn_hi_done, s)
                    dve.tensor_tensor(attn, ps_m[0][:], rdenT, ALU.mult).then_inc(attn_done, 1)
                if s % TB == 0 and s + TB < NT:
                    norm_batch_apply(b)
                if s:
                    dve.wait_ge(z_ready, s)
                    then(dve.tensor_copy(logits[:, 0, :], ps_m[2][:, ZB:ZB + E]))
                    then(dve.max(top[:, 0, :], logits[:, 0, :]))
                    then(dve.match_replace(part[:], top[:, 0, :], logits[:, 0, :], TAKEN))
                    then(dve.max(top[:, 1, :], part[:]))
                    dve.tensor_scalar(neg_top[:], top[:, 0, 0:1], -1.0, None, ALU.mult)
                    dve.match_replace(logits[:, 1, :], top[:, 1, :], part[:], TAKEN).then_inc(top_done, 1)
                if s < NT:
                    dve.wait_ge(attn_hi_done, s + 1)
                    low(flat(attn_lo[:]), attn, flat(attn_hi[:])).then_inc(attn_lo_done, 1)
                if s:
                    dve.wait_ge(e_exp_done, s)
                    then(dve.tensor_tensor(gate[:], e_exp[:, 0, :], e_exp[:, 1, :], ALU.subtract))
                    if s > 1:
                        dve.wait_ge(zgT_ready, s - 1)
                    dve.tensor_tensor(zg[:, 0:ZA].rearrange("p (e r) -> p e r", r=RANK),
                                      ps_m[1][:, 0:ZA].rearrange("p (e r) -> p e r", r=RANK),
                                      gate[:, 0:EA].unsqueeze(2).to_broadcast([P, EA, RANK]), ALU.mult)
                    dve.tensor_tensor(zg[:, ZA:D].rearrange("p (e r) -> p e r", r=RANK),
                                      ps_m[2][:, 0:ZB].rearrange("p (e r) -> p e r", r=RANK),
                                      gate[:, EA:E].unsqueeze(2).to_broadcast([P, E - EA, RANK]), ALU.mult) \
                        .then_inc(zg_done, 1)
                    then(dve.reduce_sum(gate_sum[:], gate[:], AX.X))
                    then(dve.reciprocal(gate_sum[:], gate_sum[:]))
                    if s == 1:
                        dve.wait_ge(tanh_ready, 1)
                    then(dve.tensor_scalar(gate_scale[:], gate_sum[:], tanh_g[:, 1:2], SCALING, ALU.mult, ALU.mult))
                if s % TB == 0 and s + TB < NT:
                    queries_T(b)
                    queries(b)
                if more:
                    for j in range(SB):
                        ins = softmax_sum(s + 1, j)
                    then(ins)
                    softmax_norm(s + 1)
                if s:
                    dve.wait_ge(zgT_hi_done, s)
                    low(flat(zgT_lo[:]), ps_t[0][:], flat(zgT_hi[:])).then_inc(zgT_lo_done, 1)
                if s < NT:
                    if s == 0:
                        dve.wait_ge(tanh_ready, 1)
                    dve.wait_ge(o_ready, s + 1)
                    then(dve.scalar_tensor_tensor(x[:, s, :], ps_m[0][:], tanh_g[:, 0:1], x[:, s, :], ALU.mult, ALU.add))
                    then(dve.bn_stats(stats2[:], x[:, s, :]))
                    dve.bn_aggr(mv2[:], stats2[:]).then_inc(var2_ready, 1)
                    if s % TB == TB - 1 and s + 1 < NT:
                        values(s // TB + 1)
                    dve.wait_ge(rstd2_ready, s + 1)
                    if s:
                        dve.wait_ge(x2T_ready, s)
                    dve.tensor_scalar(xn2, x[:, s, :], mv2[:, 0:1], rstd2[:], ALU.subtract, ALU.mult) \
                        .then_inc(xn2_ready, 1)
                if s:
                    dve.wait_ge(y_ready, s)
                    dve.scalar_tensor_tensor(x[:, s - 1, :], ps_m[1][:], gate_scale[:], x[:, s - 1, :],
                                             ALU.mult, ALU.add).then_inc(y_done, 1)
                if s < NT:
                    dve.wait_ge(x2T_hi_done, s + 1)
                    low(flat(x2T_lo[:]), ps_t[1][:], flat(x2T_hi[:])).then_inc(x2T_lo_done, 1)

        @block.tensor
        def _(pe):
            def transposes(bank, src):
                for c in range(DC):
                    last = pe.transpose(bank[:, P * c:P * (c + 1)], src[:, P * c:P * (c + 1)], ident[:])
                return last

            def queries_T(b):
                for t in range(TB):
                    pe.wait_ge(xn_ready, TB * b + t + 1)
                    transposes(ps_t[t], xn[:, t, :]).then_inc(xT_ready, 1)

            def queries(b):
                pe.wait_ge(xT_lo_done, TB * (b + 1))
                for j in range(2):
                    for i in range(2):
                        f = 2 * j + i
                        for c in range(DC):
                            if b == 0 and j == 0 and i == 0:
                                pe.wait_ge(wq_lo_ready, c + 1)
                            last = split3(pe, q_bank[j][:, S * i:S * (i + 1)],
                                          wq_hi[:, c, P * f:P * (f + 1)], wq_lo[:, c, P * f:P * (f + 1)],
                                          xT_hi[:, c, :], xT_lo[:, c, :], c == 0, c == DC - 1)
                    last.then_inc(q_ready, 1)

            def scores(t):
                b, h = divmod(t, TB)
                if h == 0:
                    pe.wait_ge(q_lo_done, 2 * (b + 1))
                    pe.wait_ge(kb_hi_done, b + 1)
                    pe.wait_ge(kb_lo_done, HG * (b + 1))
                cols = slice(P * h, P * (h + 1))
                for j in range(SB):
                    if j == 3:
                        pe.wait_ge(sub_done, SB * t + 1)
                    elif t:
                        pe.wait_ge(sub_done, SB * (t - 1) + (4 if j == 0 else j + 1))
                    bank = score_bank[j]
                    pe.matmul(bank[:].rearrange("p (h s) -> p h s", s=CT), ident_bf[:],
                              mask_add[:, h, :].unsqueeze(1).to_broadcast([P, 2 * HG, CT]), start=True, stop=False,
                              skip_group_check=True)
                    r = 64 * (j % 2)
                    for g in range(2):
                        c = 2 * (j // 2) + g
                        to = bank[:, GW * g:GW * (g + 1)]
                        qh, ql = qT_hi[r:r + 64, c, cols], qT_lo[r:r + 64, c, cols]
                        kh, kl = (k[r:r + 64, c, :, :].rearrange("p h s -> p (h s)") for k in (kb_hi, kb_lo))
                        pe.matmul(to, qh, kh, start=False, stop=False, skip_group_check=True)
                        pe.matmul(to, qh, kl, start=False, stop=False, skip_group_check=True)
                        last = pe.matmul(to, ql, kh, start=False, stop=g == 1, skip_group_check=True)
                    last.then_inc(s_ready, 1)

            pe.wait_ge(consts, 1)
            queries_T(0)
            pe.wait_ge(ctx_in_s, 16 * B)
            pe.wait_ge(wk_heads_ready, 1)
            for f in range(DC):
                for c in range(DC):
                    last = pe.matmul(ps_s[f // 2][:, B * CT * (f % 2):B * CT * (f % 2 + 1)],
                                     wk_heads[:, c, P * f:P * (f + 1)],
                                     ctxT[:, c, :, :].rearrange("p b s -> p (b s)"), start=c == 0, stop=c == DC - 1)
            last.then_inc(k_ready, 1)
            queries(0)
            pe.wait_ge(wv_in_s, 16)
            for b in range(B):
                for h in range(2):
                    for c in range(DC):
                        last = pe.matmul(ps_s[2][64 * h:64 * (h + 1), KV * b:KV * (b + 1)], ctxT[:, c, b, :], wv[:, c, :],
                                         start=c == 0, stop=c == DC - 1)
            last.then_inc(v_ready, 1)
            pe.wait_ge(small_in_s, 80)
            for c in range(DC):
                last = pe.matmul(ps_m[2][:, E * c:E * (c + 1)], wr[:, P * c:P * (c + 1)], keysT[:], start=True, stop=True)
            last.then_inc(m_ready, 1)
            pe.wait_ge(k_lo_done, 1)
            pe.wait_ge(vb_done, 1)
            pe.wait_ge(mask_ready, 1)
            scores(0)

            for s in range(NT + 1):
                if s + 1 < NT:
                    scores(s + 1)
                if s < NT:
                    for c in range(DC):
                        pe.wait_ge(exp_done, SB * (s + 1)) if c == 0 else None
                        if c >= 2:
                            pe.wait_ge(pT_done, DC * s + c - 1)
                        elif s and c == 0:
                            pe.wait_ge(zgT_lo_done, s - 1) if s > 1 else None
                            pe.wait_ge(q_lo_done, 2 * ((s - 1) // TB + 2)) if (s - 1) % TB == 0 and s - 1 + TB < NT else None
                        elif s:
                            pe.wait_ge(x2T_lo_done, s)
                        for i in range(4):
                            p = 4 * c + i
                            last = pe.transpose(ps_t[c % 2][:, P * i:P * (i + 1)],
                                                probs[:, s % 2, p // 2, P * (p % 2):P * (p % 2 + 1)], ident[:])
                        last.then_inc(pT_ready, 1)
                    if s:
                        pe.wait_ge(xn2_ready, s)
                    else:
                        pe.wait_ge(q_lo_done, 2)
                    if s % TB == 0:
                        pe.wait_ge(vb_done, s // TB + 1)
                    for c in range(DC):
                        pe.wait_ge(pT_done, DC * s + c + 1)
                        for i in range(4):
                            p = 4 * c + i
                            last = pe.matmul(ps_m[0][32 * i:32 * (i + 1), P * c:P * (c + 1)],
                                             vb[:, p // 2, :, :].rearrange("p h d -> p (h d)"), pT[:, p, :],
                                             start=True, stop=True)
                    last.then_inc(pv_ready, 1)
                    pe.wait_ge(rden_done, s + 1)
                    transposes(ps_t[0], rden_wide[:].rearrange("p h d -> p (h d)")).then_inc(rT_ready, 1)
                if s:
                    pe.wait_ge(x2T_lo_done, s)
                    if s == 1:
                        pe.wait_ge(w_split, 2 * DC)
                        pe.wait_ge(m_lo_done, 1)
                    else:
                        pe.wait_ge(y_done, s - 1)
                    for bank, cols in ((ps_m[1], slice(0, ZA)), (ps_m[2], slice(ZA, D + E))):
                        for c in range(DC):
                            last = split3(pe, bank[:, 0:ZA], x2T_hi[:, c, :], x2T_lo[:, c, :],
                                          aw_hi[:, c, cols], aw_lo[:, c, cols], c == 0, c == DC - 1)
                    last.then_inc(z_ready, 1)
                if s % TB == 0 and s + TB < NT:
                    pe.wait_ge(rT_done, s + 1)
                    queries_T(s // TB + 1)
                    pe.wait_ge(attn_done, s + 1)
                    queries(s // TB + 1)
                if s:
                    pe.wait_ge(zg_done, s)
                    pe.wait_ge(rT_done, s + 1) if s < NT else None
                    pe.wait_ge(xT_lo_done, TB * (s // TB + 2)) if s % TB == 0 and s + TB < NT else None
                    transposes(ps_t[0], zg).then_inc(zgT_ready, 1)
                if s < NT:
                    pe.wait_ge(attn_lo_done, s + 1)
                    if s == 0:
                        pe.wait_ge(w_split, DC)
                    if s % TB == 0 and s + TB < NT:
                        pe.wait_ge(q_lo_done, 2 * (s // TB + 1) + 1)
                    for c in range(DC):
                        last = split3(pe, ps_m[0][:], attn_hi[:, c, :], attn_lo[:, c, :],
                                      wo_hi[:, c, :], wo_lo[:, c, :], c == 0, c == DC - 1)
                    last.then_inc(o_ready, 1)
                if s:
                    pe.wait_ge(zgT_lo_done, s)
                    if s == 1:
                        pe.wait_ge(w_split, 3 * DC)
                    for c in range(DC):
                        last = split3(pe, ps_m[1][:], zgT_hi[:, c, :], zgT_lo[:, c, :],
                                      bw_hi[:, c, :], bw_lo[:, c, :], c == 0, c == DC - 1)
                    last.then_inc(y_ready, 1)
                if s < NT:
                    pe.wait_ge(xn2_ready, s + 1)
                    if s % TB == 0 and s + TB < NT:
                        pe.wait_ge(q_lo_done, 2 * (s // TB + 2))
                    elif s:
                        pass
                    pe.wait_ge(pT_done, DC * (s + 1))
                    transposes(ps_t[1], xn2).then_inc(x2T_ready, 1)


def kernel(**inputs):
    import numpy as _np
    import concourse.bacc as _bacc
    from concourse import mybir as _mybir
    from concourse.bass_utils import run_bass_kernel_spmd as _run

    i = {k: _np.asarray(a) for k, a in inputs.items()}
    laid = {
        "x": i["x"],
        "ctxT": i["ctx_4096"].transpose(0, 2, 1),
        "mask": i["mask_SxS2_bk0"],
        "g_attn": i["g_xattn"],
        "g_ffn": i["g_ffn"],
        "wqT": i["L0_xattn_w_q"].T,
        "wkT": i["L0_xattn_w_k"].T,
        "wvT": i["L0_xattn_w_v"].T,
        "woT": i["L0_xattn_w_out"].T,
        "aT": i["L0_ffn_A_w"].T,
        "bT": i["L0_ffn_B_w"].T,
        "wr": i["L0_ffn_Wq_w"],
        "keysT": i["L0_ffn_keys"].T,
    }
    nc = _bacc.Bacc("TRN2", target_bir_lowering=False, num_devices=1)
    arrays, args = {}, []
    for name, a in laid.items():
        a = _np.ascontiguousarray(a)
        arrays[f"in_{name}"] = a
        args.append(nc.dram_tensor(f"in_{name}", a.shape, _mybir.dt.from_np(a.dtype), kind="ExternalInput").ap())
    args.append(nc.dram_tensor("out_x", i["x"].shape, _mybir.dt.float32, kind="ExternalOutput").ap())
    gated_cross_attention_kernel(nc, *args)
    r = _run(nc, [arrays], core_ids=[0])
    return r.results[0]["out_x"]
```

```python
import concourse.bass as bass
from concourse import mybir
from contextlib import ExitStack


def gated_cross_attention_kernel(nc, x_in, ctxT_in, mask_in, g_attn_in, g_ffn_in,
                                 wqT_in, wkT_in, wvT_in, woT_in, aT_in, bT_in, wr_in, keysT_in,
                                 out):
    f32 = mybir.dt.float32
    f32r = mybir.dt.float32r
    bf16 = mybir.dt.bfloat16
    ALU = mybir.AluOpType
    ACT = mybir.ActivationFunctionType
    AX = mybir.AxisListType

    P = 128
    B, S, D = x_in.shape
    CT = ctxT_in.shape[3]
    KV = wkT_in.shape[2]
    E = keysT_in.shape[1]
    R = wr_in.shape[0]
    H, DH = 32, 16
    G = KV // DH
    HG = H // G
    RANK = D // E
    TB = S // P
    NT = B * TB
    DC = D // P
    GW = HG * CT
    PAIRS = H // 2
    SB = 4
    ZA = 288
    ZB = D - ZA
    EA = ZA // RANK
    EPS = 1e-5
    SCALE = DH ** -0.5
    SCALING = 32 / 16
    BIG = 3.3895313892515355e38
    WARM_UP = 64
    TAKEN = -3.0e38

    ctx = ExitStack()
    with ctx:
        def sb(name, shape, dt=f32):
            return ctx.enter_context(nc.sbuf_tensor(name, shape, dt))

        def pb(name):
            return ctx.enter_context(nc.psum_tensor(name, [P, 512], f32))

        def sem(name):
            return ctx.enter_context(nc.semaphore(name))

        x = sb("x", [P, NT, D])
        wq = sb("wq", [P, DC, D])
        wo = sb("wo", [P, DC, D])
        aw = sb("aw", [P, DC, D + E])
        bw = sb("bw", [P, DC, D])
        wq_hi, wq_lo = sb("wq_hi", [P, DC, D], f32r), sb("wq_lo", [P, DC, D], f32r)
        wo_hi, wo_lo = sb("wo_hi", [P, DC, D], f32r), sb("wo_lo", [P, DC, D], f32r)
        aw_hi, aw_lo = sb("aw_hi", [P, DC, D + E], f32r), sb("aw_lo", [P, DC, D + E], f32r)
        bw_hi, bw_lo = sb("bw_hi", [P, DC, D], f32r), sb("bw_lo", [P, DC, D], f32r)
        wk = sb("wk", [P, DC, KV])
        wv = sb("wv", [P, DC, KV])
        ctxT = sb("ctxT", [P, DC, B, CT])
        mask = sb("mask", [P, TB, CT], mask_in.dtype)
        gates = sb("gates", [P, 2])
        wr = sb("wr", [R, D])
        keysT = sb("keysT", [R, E])

        ident = sb("ident", [P, P])
        ident_bf = sb("ident_bf", [P, P], bf16)
        head_of_four = sb("head_of_four", [P, HG])
        half = sb("half", [P, 2])
        shift = sb("shift", [P, TB])
        neg_half = sb("neg_half", [P, TB])
        mask_add = sb("mask_add", [P, TB, CT], bf16)
        tanh_g = sb("tanh_g", [P, 2])

        k_all = sb("k_all", [P, B * CT])
        pick = sb("pick", [P, DC, P])
        k_hi, k_lo = sb("k_hi", [P, DC, B, CT], f32r), sb("k_lo", [P, DC, B, CT], f32r)
        kb_hi = sb("kb_hi", [P, DC, HG, CT], f32r)
        kb_lo = sb("kb_lo", [P, DC, HG, CT], f32r)
        v = sb("v", [P, B, G, DH])
        vb = sb("vb", [P, G, 2, DH])

        stats = sb("stats", [P, TB, 6])
        mv = sb("mv", [P, TB, 2])
        veps = sb("veps", [P, TB])
        rstd = sb("rstd", [P, TB])
        xn = sb("xn", [P, TB, D])
        xT_hi, xT_lo = sb("xT_hi", [P, DC, S], f32r), sb("xT_lo", [P, DC, S], f32r)
        qT_hi, qT_lo = sb("qT_hi", [P, DC, S], f32r), sb("qT_lo", [P, DC, S], f32r)

        probs = sb("probs", [P, 2, G, GW])
        smax = sb("smax", [P, SB, 2 * HG])
        den = sb("den", [P, SB, 2 * HG])
        rden = sb("rden", [P, SB, 2 * HG])
        rden_wide = wk[:].rearrange("p c (a d) -> p (c a) d", d=DH)
        pT = sb("pT", [P, PAIRS, P])
        rdenT, attn, xn2, zg = (wq[:, c, :] for c in range(DC))
        attn_hi, attn_lo = sb("attn_hi", [P, DC, P], f32r), sb("attn_lo", [P, DC, P], f32r)

        stats2 = sb("stats2", [P, 6])
        mv2 = sb("mv2", [P, 2])
        veps2 = sb("veps2", [P, 1])
        rstd2 = sb("rstd2", [P, 1])
        x2T_hi, x2T_lo = sb("x2T_hi", [P, DC, P], f32r), sb("x2T_lo", [P, DC, P], f32r)
        logits = sb("logits", [P, 2, E])
        part = sb("part", [P, E])
        top = sb("top", [P, 2, 8])
        neg_top = sb("neg_top", [P, 1])
        e_exp = sb("e_exp", [P, 2, E])
        gate = sb("gate", [P, E])
        gate_sum = sb("gate_sum", [P, 1])
        gate_scale = sb("gate_scale", [P, 1])
        zgT_hi, zgT_lo = sb("zgT_hi", [P, DC, P], f32r), sb("zgT_lo", [P, DC, P], f32r)

        ps_s = [pb(f"ps_s{i}") for i in range(3)]
        ps_t = [pb(f"ps_t{i}") for i in range(2)]
        ps_m = [pb(f"ps_m{i}") for i in range(3)]
        score_bank = [ps_s[0], ps_s[1], ps_s[2], ps_s[0]]

        q_bank = [ps_m[0], ps_t[1]]
        pT_bank = [[ps_t[1], ps_t[0], ps_t[0], ps_t[1]], [ps_t[1], ps_t[0], ps_t[1], ps_t[0]]] * (B - 1) \
            + [[ps_t[1], ps_t[0], ps_s[1], ps_s[2]]] * TB
        pT_bank[1] = [ps_t[1], ps_m[2], ps_t[1], ps_m[2]]
        rT_bank = [ps_t[0], ps_t[1]]
        x2T_bank = [ps_t[0], ps_t[1]] * (B - 1) + [ps_m[1], None]
        zgT_bank = ps_t[0]
        out_bank = [ps_m[1]] * (NT - 2) + [ps_s[0], ps_s[1]]
        z_banks = [(ps_m[1], ps_m[2])] * (NT - 1) + [(ps_s[0], ps_s[2])]
        y_bank = [ps_m[2]] * (NT - 1) + [ps_s[1]]

        def xT_bank(b, t):
            return ps_t[0] if b == 1 else ps_t[t]

        last_banks = {"x2T": (ps_t[1], ps_m[0]), "zgT": (ps_t[0], ps_m[0])}

        def bank_probs(t, j):
            g0 = 4 * (j // 2) + j % 2
            return probs[:, t % 2, g0:g0 + 3:2, :]

        x_in_s = [sem(f"x_loaded{b}") for b in range(B)]
        wq_in_s = [sem(f"wq_loaded{j}") for j in range(2)]
        wo_in_s, aw_in_s, bw_in_s = (sem(n) for n in ("wo_loaded", "aw_loaded", "bw_loaded"))
        ctx_in_s, wk_in_s, wv_in_s, small_in_s = (sem(n) for n in ("ctx_loaded", "wk_loaded", "wv_loaded", "small_loaded"))
        pool_step = sem("pool_step")
        consts = sem("consts_ready")
        tanh_ready = sem("tanh_ready")
        mask_ready = sem("mask_ready")
        k_all_ready, k_all_done = sem("k_all_ready"), sem("k_all_done")
        wq_hi_ready, wq_lo_ready, wo_hi_ready = sem("wq_hi_ready"), sem("wq_lo_ready"), sem("wo_hi_ready")
        w_split = sem("w_split")
        k_ready, v_ready, m_ready = sem("k_ready"), sem("v_ready"), sem("m_ready")
        k_hi_done, k_lo_done, v_done, m_hi_done, m_lo_done = (sem(n) for n in ("k_hi_done", "k_lo_done", "v_done", "m_hi_done", "m_lo_done"))
        kb_done, vb_done = sem("kb_done"), sem("vb_done")
        dve_step = sem("dve_step")
        var_ready, rstd_ready = sem("var_ready"), sem("rstd_ready")
        xn_ready, xT_ready, xT_hi_done, xT_lo_done = (sem(n) for n in ("xn_ready", "xT_ready", "xT_hi_done", "xT_lo_done"))
        q_ready, q_hi_done, q_lo_done = sem("q_ready"), sem("q_hi_done"), sem("q_lo_done")
        s_ready, sub_done, exp_done = sem("scores_ready"), sem("sub_done"), sem("exp_done")
        rden_ready, rden_done = sem("rden_ready"), sem("rden_done")
        pT_ready, pT_done = sem("pT_ready"), sem("pT_done")
        pv_ready, rT_ready, rT_done, attn_done = (sem(n) for n in ("pv_ready", "rdenT_ready", "rdenT_done", "attn_done"))
        attn_hi_done, attn_lo_done = sem("attn_hi_done"), sem("attn_lo_done")
        o_ready, x2_done = sem("o_ready"), sem("x2_done")
        var2_ready, rstd2_ready, xn2_ready = sem("var2_ready"), sem("rstd2_ready"), sem("xn2_ready")
        x2T_ready, x2T_hi_done, x2T_lo_done = sem("x2T_ready"), sem("x2T_hi_done"), sem("x2T_lo_done")
        za_ready, zb_ready, top_done, e_exp_done, zg_done = sem("za_ready"), sem("zb_ready"), sem("top_done"), sem("e_exp_done"), sem("zg_done")
        zgT_ready, zgT_hi_done, zgT_lo_done = sem("zgT_ready"), sem("zgT_hi_done"), sem("zgT_lo_done")
        last_ready, last_hi_done, last_lo_done = sem("last_ready"), sem("last_hi_done"), sem("last_lo_done")
        y_ready, y_done, stored = sem("y_ready"), sem("y_done"), sem("stored")

        def split3(pe, to, lhs_hi, lhs_lo, rhs_hi, rhs_lo, first, last):
            pe.matmul(to, lhs_hi, rhs_hi, start=first, stop=False)
            pe.matmul(to, lhs_hi, rhs_lo, start=False, stop=False)
            return pe.matmul(to, lhs_lo, rhs_hi, start=False, stop=last)

        block = ctx.enter_context(nc.Block())

        @block.sync
        def _(sp):
            xv = x_in.rearrange("b (t p) d -> p (b t) d", p=P)
            ov = out.rearrange("b (t p) d -> p (b t) d", p=P)
            sp.dma_start(x[:, 0:TB, :], xv[:, 0:TB, :]).then_inc(x_in_s[0], 16)
            for j in range(2):
                sp.dma_start(wq[:, 2 * j:2 * j + 2, :], wqT_in[:, 2 * j:2 * j + 2, :]).then_inc(wq_in_s[j], 16)
            sp.dma_start(wr[:, :], wr_in).then_inc(small_in_s, 16)
            sp.dma_start(keysT[:, :], keysT_in).then_inc(small_in_s, 16)
            sp.dma_start(mask[:, :, :], mask_in.rearrange("(t p) s -> p t s", p=P)).then_inc(small_in_s, 16)
            sp.dma_start(gates[:, 0:1], g_attn_in.partition_broadcast(P)).then_inc(small_in_s, 16)
            sp.dma_start(gates[:, 1:2], g_ffn_in.partition_broadcast(P)).then_inc(small_in_s, 16)
            sp.dma_start(x[:, TB:2 * TB, :], xv[:, TB:2 * TB, :]).then_inc(x_in_s[1], 16)
            sp.dma_start(wo[:, :, :], woT_in).then_inc(wo_in_s, 16)
            sp.dma_start(aw[:, :, 0:D], aT_in).then_inc(aw_in_s, 16)
            sp.dma_start(bw[:, :, :], bT_in).then_inc(bw_in_s, 16)
            for b in range(2, B):
                sp.dma_start(x[:, TB * b:TB * (b + 1), :], xv[:, TB * b:TB * (b + 1), :]).then_inc(x_in_s[b], 16)
            for t in range(NT):
                sp.wait_ge(y_done, t + 1)
                sp.dma_start(ov[:, t:t + 1, :], x[:, t:t + 1, :]).then_inc(stored, 16)
            sp.wait_ge(stored, 16 * NT)

        @block.gpsimd
        def _(pool):
            step = [0]

            def then(ins):
                step[0] += 1
                ins.then_inc(pool_step, 1)
                pool.wait_ge(pool_step, step[0])

            def signal(ins, to, value):
                ins.then_inc(to, 1)
                pool.wait_ge(to, value)

            then(pool.memset(neg_half[:], -0.5))
            then(pool.memset(ident[:], 0.0))
            then(pool.affine_select(out=ident[:], in_=ident[:], compare_op=ALU.not_equal, fill=1.0,
                                    base=0, pattern=[[-1, P]], channel_multiplier=1))
            signal(pool.tensor_copy(ident_bf[:], ident[:]), consts, 1)
            then(pool.memset(pick[:], 0.0))
            signal(pool.affine_select(out=pick[:].rearrange("p c (g h d) -> p (c g) h d", g=2, h=HG),
                                      in_=pick[:].rearrange("p c (g h d) -> p (c g) h d", g=2, h=HG),
                                      compare_op=ALU.not_equal, fill=1.0, base=0,
                                      pattern=[[-DH, G], [0, HG], [-1, DH]], channel_multiplier=1), consts, 2)

            def inv_sqrt(out_, veps_, var):
                then(pool.tensor_scalar(veps_, var, EPS, 0.0, ALU.add, ALU.add))
                return pool.tensor_tensor(out_, veps_, neg_half[:, 0:veps_.shape[1]], ALU.pow)

            def rstd_batch(b):
                pool.wait_ge(var_ready, b + 1)
                if b:
                    pool.wait_ge(xn_ready, TB * b)
                then(inv_sqrt(rstd[:], veps[:], mv[:, :, 1]))
                then(pool.tensor_tensor(shift[:], mv[:, :, 0], rstd[:], ALU.mult))
                signal(pool.tensor_scalar(shift[:], shift[:], -1.0, 0.0, ALU.mult, ALU.add), rstd_ready, b + 1)

            def split_weight(hi, lo, w, loaded, n):
                pool.wait_ge(loaded, 16)
                for c in range(DC):
                    then(pool.tensor_scalar(hi[:, c, 0:D], w[:, c, 0:D], 1.0, 0.0, ALU.mult, ALU.add))
                    signal(pool.tensor_tensor(lo[:, c, 0:D], w[:, c, 0:D], hi[:, c, 0:D].bitcast(f32),
                                              ALU.subtract), w_split, DC * n + c + 1)

            def keys(b):
                if b:
                    pool.wait_ge(s_ready, SB * TB * b)
                for part_of, (to, k) in enumerate(((kb_hi, k_hi), (kb_lo, k_lo))):
                    for hh in range(HG):
                        signal(pool.tensor_scalar(to[:, :, hh, :], k[:, :, b, :].bitcast(f32),
                                                  head_of_four[:, hh:hh + 1], 0.0, ALU.mult, ALU.add),
                               kb_done, HG * (2 * b + part_of) + hh + 1)

            def values(b):
                if b:
                    pool.wait_ge(pv_ready, TB * b)
                for h in range(2):
                    signal(pool.tensor_scalar(vb[:, :, h, :], v[:, b, :, :], half[:, h:h + 1], 0.0,
                                              ALU.mult, ALU.add), vb_done, 2 * b + h + 1)

            rstd_batch(0)
            then(pool.memset(half[:], 1.0))
            then(pool.affine_select(out=half[:], in_=half[:], compare_op=ALU.is_ge, fill=0.0,
                                    base=0, pattern=[[-CT, 2]], channel_multiplier=1))
            signal(pool.affine_select(out=half[:], in_=half[:], compare_op=ALU.is_ge, fill=0.0,
                                      base=CT - 1, pattern=[[CT, 2]], channel_multiplier=-1), consts, 3)
            then(pool.memset(head_of_four[:], SCALE))
            for g2 in range(2):
                rows = head_of_four[64 * g2:64 * (g2 + 1), :]
                then(pool.affine_select(out=rows, in_=rows, compare_op=ALU.is_ge, fill=0.0,
                                        base=0, pattern=[[-DH, HG]], channel_multiplier=1))
                signal(pool.affine_select(out=rows, in_=rows, compare_op=ALU.is_ge, fill=0.0,
                                          base=DH - 1, pattern=[[DH, HG]], channel_multiplier=-1), consts, 4 + g2)

            pool.wait_ge(k_lo_done, 1)
            keys(0)
            rstd_batch(1)
            for c in range(DC):
                pool.wait_ge(wo_hi_ready, c + 1)
                signal(pool.tensor_tensor(wo_lo[:, c, :], wo[:, c, :], wo_hi[:, c, :].bitcast(f32), ALU.subtract),
                       w_split, c + 1)
            pool.wait_ge(v_done, 1)
            values(0)
            split_weight(aw_hi, aw_lo, aw, aw_in_s, 1)
            for s in range(NT):
                b = s // TB
                if s % TB == 0 and b + 1 < B:
                    keys(b + 1)
                if s % TB == 1 and b + 1 < B:
                    values(b + 1)
                if s % TB == 0 and b + 2 < B:
                    rstd_batch(b + 2)
                pool.wait_ge(var2_ready, s + 1)
                signal(inv_sqrt(rstd2[:], veps2[:], mv2[:, 1:2]), rstd2_ready, s + 1)
                if s == 0:
                    split_weight(bw_hi, bw_lo, bw, bw_in_s, 2)

        @block.scalar
        def _(act):
            act.dma_start(ctxT[:, :, :, :], ctxT_in).then_inc(ctx_in_s, 16)
            act.dma_start(wk[:, :, :], wkT_in).then_inc(wk_in_s, 16)
            act.dma_start(wv[:, :, :], wvT_in).then_inc(wv_in_s, 16)

            def copy_hi(to, src, done):
                act.copy(to, src).then_inc(done, 1)

            def flat(a):
                return a.rearrange("p c n -> p (c n)")

            def normalise(b, tiles=range(TB)):
                act.wait_ge(rstd_ready, b + 1)
                if b:
                    act.wait_ge(xT_ready, TB * b)
                for t in tiles:
                    act.activation(xn[:, t, :], x[:, TB * b + t, :], ACT.Identity, scale=rstd[:, t:t + 1],
                                   bias=shift[:, t:t + 1]).then_inc(xn_ready, 1)

            def tokens_T(b, t):
                act.wait_ge(xT_ready, TB * b + t + 1)
                copy_hi(xT_hi[:, :, P * t:P * (t + 1)], xT_bank(b, t)[:].rearrange("p (c n) -> p c n", c=DC), xT_hi_done)

            def queries(b, j):
                act.wait_ge(q_ready, 2 * b + j + 1)
                if b:
                    act.wait_ge(s_ready, SB * TB * b)
                copy_hi(qT_hi[:, 2 * j:2 * j + 2, :], q_bank[j][:].rearrange("p (c n) -> p c n", c=2), q_hi_done)

            def exps(t, j):
                act.wait_ge(sub_done, SB * t + j + 1)
                view = bank_probs(t, j)
                act.activation(view, view, ACT.Exp).then_inc(exp_done, 1)

            def probs_T(t, c):
                act.wait_ge(pT_ready, DC * t + c + 1)
                if t and c == 0:
                    act.wait_ge(pv_ready, t)
                act.copy(pT[:, 4 * c:4 * (c + 1), :].rearrange("p a n -> p (a n)"), pT_bank[t][c][:]).then_inc(pT_done, 1)

            def denominators(t):
                act.wait_ge(rden_ready, t + 1)
                if t:
                    act.wait_ge(rT_ready, t)
                act.copy(rden_wide, rden[:].rearrange("p j h -> p (j h)").unsqueeze(2)
                         .to_broadcast([P, H, DH])).then_inc(rden_done, 1)

            def attention(t):
                act.wait_ge(rT_ready, t + 1)
                if t:
                    act.wait_ge(attn_done, t)
                act.copy(rdenT, rT_bank[t % 2][:]).then_inc(rT_done, 1)

            def attention_hi(t):
                act.wait_ge(attn_done, t + 1)
                if t:
                    act.wait_ge(o_ready, t)
                act.copy(flat(attn_hi[:]), attn).then_inc(attn_hi_done, 1)

            def router(t):
                act.wait_ge(top_done, t + 1)
                act.activation(e_exp[:], logits[:], ACT.Exp, bias=neg_top[:]).then_inc(e_exp_done, 1)

            def gated_T(t):
                act.wait_ge(zgT_ready, t + 1)
                if t:
                    act.wait_ge(y_ready, t)
                copy_hi(flat(zgT_hi[:]), zgT_bank[:], zgT_hi_done)

            def tokens2_T(t):
                act.wait_ge(x2T_ready, t + 1)
                if t:
                    act.wait_ge(za_ready, t)
                    act.wait_ge(zb_ready, t)
                copy_hi(flat(x2T_hi[:]), x2T_bank[t][:], x2T_hi_done)

            def split_wq(j):
                act.wait_ge(wq_in_s[j], 16)
                for c in range(2 * j, 2 * j + 2):
                    copy_hi(wq_hi[:, c, :], wq[:, c, :], wq_hi_ready)

            def last_half(name, hi, h, n):
                act.wait_ge(last_ready, n)
                half_of = slice(2 * P * h, 2 * P * (h + 1))
                copy_hi(flat(hi[:])[:, half_of], last_banks[name][h][:, half_of], last_hi_done)

            normalise(0)
            split_wq(0)
            split_wq(1)
            act.wait_ge(k_all_ready, 1)
            act.copy(k_all[:], ps_s[0][:, 0:B * CT]).then_inc(k_all_done, 1)
            tokens_T(0, 0)
            tokens_T(0, 1)
            act.wait_ge(k_ready, 1)
            for j in range(2):
                copy_hi(k_hi[:, 2 * j:2 * j + 2, :, :].rearrange("p c b s -> p (c b s)"), ps_s[1 + j][:], k_hi_done)
            act.wait_ge(wo_in_s, 16)
            for c in range(DC):
                copy_hi(wo_hi[:, c, :], wo[:, c, :], wo_hi_ready)
            for j in range(2):
                queries(0, j)
            act.wait_ge(small_in_s, 80)
            act.activation(tanh_g[:], gates[:], ACT.Tanh).then_inc(tanh_ready, 1)
            act.wait_ge(m_ready, 1)
            copy_hi(aw_hi[:, :, D:D + E], ps_m[2][:, 0:DC * E].rearrange("p (c e) -> p c e", c=DC), m_hi_done)
            normalise(1)
            exps(0, 0)
            exps(0, 1)
            tokens_T(1, 0)
            exps(0, 2)
            probs_T(0, 0)
            exps(0, 3)
            act.wait_ge(v_ready, 1)
            act.copy(v[:].rearrange("p b g d -> p (b g d)"), ps_m[1][:]).then_inc(v_done, 1)
            tokens_T(1, 1)
            probs_T(0, 1)
            exps(1, 0)
            exps(1, 1)
            denominators(0)
            queries(1, 0)
            probs_T(0, 2)
            exps(1, 2)
            probs_T(0, 3)

            for s in range(NT - TB):
                b = s // TB
                if s > 1:
                    probs_T(s, 0)
                    probs_T(s, 1)
                if s and s % TB == 0:
                    exps(s + 1, 2)
                    tokens2_T(s - 1)
                    exps(s + 1, 3)
                    queries(b + 1, 0)
                if s % TB:
                    exps(s + 1, 3)
                if s > 1:
                    probs_T(s, 2)
                    probs_T(s, 3)
                if s == 2:
                    denominators(2)
                attention(s)
                if s == 0:
                    exps(1, 3)
                if s % TB and b + 2 < B:
                    normalise(b + 2, (0,))
                if s:
                    router(s - 1)
                if s % TB and b + 2 < B:
                    normalise(b + 2, (1,))
                attention_hi(s)
                if s == 0:
                    queries(1, 1)
                    probs_T(1, 0)
                    exps(2, 0)
                    probs_T(1, 1)
                    tokens2_T(0)
                    exps(2, 1)
                    probs_T(1, 2)
                    probs_T(1, 3)
                    denominators(1)
                    exps(2, 2)
                elif s % TB == 0:
                    queries(b + 1, 1)
                    gated_T(s - 1)
                    denominators(s + 1)
                    exps(s + 2, 0)
                    exps(s + 2, 1)
                    tokens2_T(s)
                    exps(s + 2, 2)
                else:
                    if b + 2 < B:
                        tokens_T(b + 2, 0)
                        tokens_T(b + 2, 1)
                    if s > 1:
                        denominators(s + 1)
                    gated_T(s - 1)
                    exps(s + 2, 0)
                    exps(s + 2, 1)

            t = NT - 2
            probs_T(t, 0)
            probs_T(t, 1)
            tokens2_T(t - 1)
            probs_T(t, 2)
            probs_T(t, 3)
            attention(t)
            exps(t + 1, 2)
            exps(t + 1, 3)
            attention_hi(t)
            router(t - 1)
            denominators(t + 1)
            probs_T(t + 1, 0)
            probs_T(t + 1, 1)
            probs_T(t + 1, 2)
            probs_T(t + 1, 3)
            attention(t + 1)
            gated_T(t - 1)
            attention_hi(t + 1)
            tokens2_T(t)
            act.wait_ge(za_ready, t + 1)
            act.wait_ge(zb_ready, t + 1)
            for h in range(2):
                last_half("x2T", x2T_hi, h, h + 1)
            router(t)
            gated_T(t)
            router(t + 1)
            act.wait_ge(y_ready, t + 1)
            for h in range(2):
                last_half("zgT", zgT_hi, h, h + 3)

        @block.vector
        def _(dve):
            step = [0]

            def then(ins):
                step[0] += 1
                ins.then_inc(dve_step, 1)
                dve.wait_ge(dve_step, step[0])

            def low(to, whole, hi):
                return dve.tensor_tensor(to, whole, hi.bitcast(f32), ALU.subtract)

            def flat(a):
                return a.rearrange("p c n -> p (c n)")

            def batch_stats(b):
                dve.wait_ge(x_in_s[b], 16)
                if b:
                    dve.wait_ge(rstd_ready, b)
                for t in range(TB):
                    dve.bn_stats(stats[:, t, :], x[:, TB * b + t, :]).then_inc(dve_step, 1)
                step[0] += TB
                dve.wait_ge(dve_step, step[0])
                for t in range(TB):
                    ins = dve.bn_aggr(mv[:, t, :], stats[:, t, :])
                ins.then_inc(var_ready, 1)

            def tokens_T(b, t):
                dve.wait_ge(xT_hi_done, TB * b + t + 1)
                low(xT_lo[:, :, P * t:P * (t + 1)], xT_bank(b, t)[:].rearrange("p (c n) -> p c n", c=DC),
                    xT_hi[:, :, P * t:P * (t + 1)]).then_inc(xT_lo_done, 1)

            def queries(b, j):
                dve.wait_ge(q_hi_done, 2 * b + j + 1)
                low(qT_lo[:, 2 * j:2 * j + 2, :], q_bank[j][:].rearrange("p (c n) -> p c n", c=2),
                    qT_hi[:, 2 * j:2 * j + 2, :]).then_inc(q_lo_done, 1)

            max_step, scale_step, x2_step = {}, [0], [0]

            def row_max(t, j):
                dve.wait_ge(s_ready, SB * t + j + 1)
                dve.reduce_max(smax[:, j, :], score_bank[j][:].rearrange("p (h s) -> p h s", s=CT), AX.X) \
                    .then_inc(dve_step, 1)
                step[0] += 1
                max_step[j] = step[0]

            def take_off(t, j):
                dve.wait_ge(dve_step, max_step[j])
                if t >= 2 and j == 0:
                    dve.wait_ge(pT_ready, DC * (t - 1))
                dve.tensor_tensor(bank_probs(t, j).rearrange("p g (h s) -> p g h s", s=CT),
                                  score_bank[j][:].rearrange("p (g h s) -> p g h s", g=2, s=CT),
                                  smax[:, j, :].rearrange("p (g h) -> p g h", g=2).unsqueeze(3)
                                  .to_broadcast([P, 2, HG, CT]), ALU.subtract).then_inc(sub_done, 1)

            def softmax_sums(t, j):
                if t and j == 0:
                    dve.wait_ge(rden_done, t)
                dve.wait_ge(exp_done, SB * t + j + 1)
                ins = dve.reduce_sum(den[:, 2 * (j // 2):2 * (j // 2) + 2, (j % 2) * HG:(j % 2 + 1) * HG],
                                     bank_probs(t, j).rearrange("p g (h s) -> p g h s", s=CT), AX.X)
                if j == SB - 1:
                    then(ins)
                    dve.reciprocal(rden[:], den[:]).then_inc(rden_ready, 1)

            def attention(t):
                dve.wait_ge(pv_ready, t + 1)
                dve.wait_ge(rT_done, t + 1)
                if t:
                    dve.wait_ge(attn_hi_done, t)
                dve.tensor_tensor(attn, ps_m[0][:], rdenT, ALU.mult).then_inc(attn_done, 1)

            def attention_lo(t):
                dve.wait_ge(attn_hi_done, t + 1)
                low(flat(attn_lo[:]), attn, flat(attn_hi[:])).then_inc(attn_lo_done, 1)

            def router(t):
                dve.wait_ge(zb_ready, t + 1)
                then(dve.tensor_copy(logits[:, 0, :], z_banks[t][1][:, ZB:ZB + E]))
                then(dve.max(top[:, 0, :], logits[:, 0, :]))
                then(dve.match_replace(part[:], top[:, 0, :], logits[:, 0, :], TAKEN))
                then(dve.max(top[:, 1, :], part[:]))
                dve.tensor_scalar(neg_top[:], top[:, 0, 0:1], -1.0, None, ALU.mult)
                dve.match_replace(logits[:, 1, :], top[:, 1, :], part[:], TAKEN).then_inc(top_done, 1)

            def gating(t):
                dve.wait_ge(e_exp_done, t + 1)
                then(dve.tensor_tensor(gate[:], e_exp[:, 0, :], e_exp[:, 1, :], ALU.subtract))
                dve.wait_ge(za_ready, t + 1)
                if t:
                    dve.wait_ge(zgT_ready, t)
                dve.tensor_tensor(zg[:, 0:ZA].rearrange("p (e r) -> p e r", r=RANK),
                                  z_banks[t][0][:, 0:ZA].rearrange("p (e r) -> p e r", r=RANK),
                                  gate[:, 0:EA].unsqueeze(2).to_broadcast([P, EA, RANK]), ALU.mult)
                dve.tensor_tensor(zg[:, ZA:D].rearrange("p (e r) -> p e r", r=RANK),
                                  z_banks[t][1][:, 0:ZB].rearrange("p (e r) -> p e r", r=RANK),
                                  gate[:, EA:E].unsqueeze(2).to_broadcast([P, E - EA, RANK]), ALU.mult) \
                    .then_inc(zg_done, 1)

            def gate_sums(t):
                then(dve.reduce_sum(gate_sum[:], gate[:], AX.X))
                then(dve.reciprocal(gate_sum[:], gate_sum[:]))
                dve.tensor_scalar(gate_scale[:], gate_sum[:], tanh_g[:, 1:2], SCALING, ALU.mult, ALU.mult) \
                    .then_inc(dve_step, 1)
                step[0] += 1
                scale_step[0] = step[0]

            def gated_T(t):
                dve.wait_ge(zgT_hi_done, t + 1)
                low(flat(zgT_lo[:]), zgT_bank[:], flat(zgT_hi[:])).then_inc(zgT_lo_done, 1)

            def residual(t):
                dve.wait_ge(o_ready, t + 1)
                dve.scalar_tensor_tensor(x[:, t, :], out_bank[t][:], tanh_g[:, 0:1], x[:, t, :], ALU.mult, ALU.add) \
                    .then_inc(dve_step, 1)
                step[0] += 1
                x2_step[0] = step[0]

            def stats_of_residual(t):
                dve.wait_ge(dve_step, x2_step[0])
                then(dve.bn_stats(stats2[:], x[:, t, :]))
                dve.bn_aggr(mv2[:], stats2[:]).then_inc(var2_ready, 1)

            def normalise2(t):
                dve.wait_ge(rstd2_ready, t + 1)
                if t:
                    dve.wait_ge(x2T_ready, t)
                dve.tensor_scalar(xn2, x[:, t, :], mv2[:, 0:1], rstd2[:], ALU.subtract, ALU.mult) \
                    .then_inc(xn2_ready, 1)

            def tokens2_T(t):
                dve.wait_ge(x2T_hi_done, t + 1)
                low(flat(x2T_lo[:]), x2T_bank[t][:], flat(x2T_hi[:])).then_inc(x2T_lo_done, 1)

            def result(t):
                dve.wait_ge(y_ready, t + 1)
                dve.wait_ge(dve_step, scale_step[0])
                dve.scalar_tensor_tensor(x[:, t, :], y_bank[t][:], gate_scale[:], x[:, t, :],
                                         ALU.mult, ALU.add).then_inc(y_done, 1)

            def last_half(name, hi, lo, h, n):
                dve.wait_ge(last_hi_done, n)
                half_of = slice(2 * P * h, 2 * P * (h + 1))
                low(flat(lo[:])[:, half_of], last_banks[name][h][:, half_of], flat(hi[:])[:, half_of]) \
                    .then_inc(last_lo_done, 1)

            batch_stats(0)
            for c in range(DC):
                dve.wait_ge(wq_hi_ready, c + 1)
                low(wq_lo[:, c, :], wq[:, c, :], wq_hi[:, c, :]).then_inc(wq_lo_ready, 1)
            tokens_T(0, 0)
            tokens_T(0, 1)
            for j in range(2):
                dve.wait_ge(k_hi_done, j + 1)
                ins = low(k_lo[:, 2 * j:2 * j + 2, :, :].rearrange("p c b s -> p (c b s)"), ps_s[1 + j][:],
                          k_hi[:, 2 * j:2 * j + 2, :, :].rearrange("p c b s -> p (c b s)"))
            ins.then_inc(k_lo_done, 1)
            batch_stats(1)
            dve.wait_ge(small_in_s, 80)
            dve.tensor_scalar(mask_add[:], mask[:], 1.0, BIG, ALU.subtract, ALU.mult).then_inc(mask_ready, 1)
            for j in range(2):
                queries(0, j)
            dve.wait_ge(tanh_ready, 1)
            dve.wait_ge(m_hi_done, 1)
            low(aw_lo[:, :, D:D + E], ps_m[2][:, 0:DC * E].rearrange("p (c e) -> p c e", c=DC),
                aw_hi[:, :, D:D + E]).then_inc(m_lo_done, 1)
            for j in range(SB):
                row_max(0, j)
                take_off(0, j)
                if j == 2:
                    tokens_T(1, 0)
            softmax_sums(0, 0)
            softmax_sums(0, 1)
            for j in range(SB):
                row_max(1, j)
                take_off(1, j)
                if j == 0:
                    tokens_T(1, 1)
                    softmax_sums(0, 2)
                if j == 1:
                    softmax_sums(0, 3)
                if j == 2:
                    queries(1, 0)

            for s in range(NT - TB):
                b = s // TB
                if s and s % TB == 0:
                    tokens2_T(s - 1)
                    if s == 2:
                        softmax_sums(2, 2)
                        softmax_sums(2, 3)
                    softmax_sums(s + 1, 0)
                    softmax_sums(s + 1, 1)
                    queries(b + 1, 0)
                    softmax_sums(s + 1, 2)
                    softmax_sums(s + 1, 3)
                elif s:
                    for j in range(2 if s == 1 else SB):
                        softmax_sums(s + 1, j)
                if s:
                    router(s - 1)
                attention(s)
                if s:
                    gating(s - 1)
                attention_lo(s)
                if s == 0:
                    softmax_sums(1, 0)
                    queries(1, 1)
                    batch_stats(2)
                elif s % TB == 0:
                    gate_sums(s - 1)
                    queries(b + 1, 1)
                    gated_T(s - 1)
                    if b + 2 < B:
                        batch_stats(b + 2)
                if s % TB == 0:
                    residual(s)
                    if s == 0:
                        stats_of_residual(s)
                    row_max(s + 2, 0)
                    take_off(s + 2, 0)
                    if s:
                        stats_of_residual(s)
                    else:
                        normalise2(s)
                    row_max(s + 2, 1)
                    if s:
                        normalise2(s)
                    take_off(s + 2, 1)
                    if s == 0:
                        tokens2_T(s)
                        softmax_sums(1, 1)
                        softmax_sums(1, 2)
                        softmax_sums(1, 3)
                    row_max(s + 2, 2)
                    take_off(s + 2, 2)
                    if s:
                        tokens2_T(s)
                    row_max(s + 2, 3)
                    take_off(s + 2, 3)
                    if s:
                        result(s - 1)
                else:
                    if b + 2 < B:
                        tokens_T(b + 2, 0)
                        tokens_T(b + 2, 1)
                    gate_sums(s - 1)
                    row_max(s + 2, 0)
                    take_off(s + 2, 0)
                    gated_T(s - 1)
                    row_max(s + 2, 1)
                    residual(s)
                    take_off(s + 2, 1)
                    stats_of_residual(s)
                    row_max(s + 2, 2)
                    take_off(s + 2, 2)
                    normalise2(s)
                    result(s - 1)
                    row_max(s + 2, 3)
                    take_off(s + 2, 3)

            t = NT - 2
            tokens2_T(t - 1)
            softmax_sums(t + 1, 0)
            attention(t)
            softmax_sums(t + 1, 1)
            attention_lo(t)
            router(t - 1)
            softmax_sums(t + 1, 2)
            gating(t - 1)
            softmax_sums(t + 1, 3)
            gate_sums(t - 1)
            residual(t)
            stats_of_residual(t)
            normalise2(t)
            gated_T(t - 1)
            attention(t + 1)
            attention_lo(t + 1)
            tokens2_T(t)
            result(t - 1)
            residual(t + 1)
            stats_of_residual(t + 1)
            normalise2(t + 1)
            router(t)
            for h in range(2):
                last_half("x2T", x2T_hi, x2T_lo, h, h + 1)
            gating(t)
            gate_sums(t)
            gated_T(t)
            router(t + 1)
            gating(t + 1)
            result(t)
            for h in range(2):
                last_half("zgT", zgT_hi, zgT_lo, h, h + 3)
            gate_sums(t + 1)
            result(t + 1)

        @block.tensor
        def _(pe):
            def transposes(bank, src):
                for c in range(DC):
                    last = pe.transpose(bank[:, P * c:P * (c + 1)], src[:, P * c:P * (c + 1)], ident[:])
                return last

            def tokens_T(b, t):
                pe.wait_ge(xn_ready, TB * b + t + 1)
                if b == 1 and t:
                    pe.wait_ge(xT_lo_done, TB * b + t)
                transposes(xT_bank(b, t), xn[:, t, :]).then_inc(xT_ready, 1)

            def queries(b, j):
                pe.wait_ge(xT_lo_done, TB * (b + 1))
                for i in range(2):
                    f = 2 * j + i
                    for c in range(DC):
                        if b == 0 and j == 0 and i == 0:
                            pe.wait_ge(wq_lo_ready, c + 1)
                        last = split3(pe, q_bank[j][:, S * i:S * (i + 1)],
                                      wq_hi[:, c, P * f:P * (f + 1)], wq_lo[:, c, P * f:P * (f + 1)],
                                      xT_hi[:, c, :], xT_lo[:, c, :], c == 0, c == DC - 1)
                last.then_inc(q_ready, 1)

            def scores(t, j):
                b, h = divmod(t, TB)
                if h == 0 and j == 0:
                    pe.wait_ge(q_lo_done, 2 * (b + 1))
                    pe.wait_ge(kb_done, 2 * HG * (b + 1))
                cols = slice(P * h, P * (h + 1))
                if j == 3:
                    pe.wait_ge(sub_done, SB * t + 1)
                elif t:
                    pe.wait_ge(sub_done, SB * (t - 1) + (4 if j == 0 else j + 1))
                bank = score_bank[j]
                pe.matmul(bank[:].rearrange("p (h s) -> p h s", s=CT), ident_bf[:],
                          mask_add[:, h, :].unsqueeze(1).to_broadcast([P, 2 * HG, CT]), start=True, stop=False,
                          skip_group_check=True)
                r = 64 * (j % 2)
                for g in range(2):
                    c = 2 * (j // 2) + g
                    to = bank[:, GW * g:GW * (g + 1)]
                    qh, ql = qT_hi[r:r + 64, c, cols], qT_lo[r:r + 64, c, cols]
                    kh, kl = (k[r:r + 64, c, :, :].rearrange("p h s -> p (h s)") for k in (kb_hi, kb_lo))
                    pe.matmul(to, qh, kh, start=False, stop=False, skip_group_check=True)
                    pe.matmul(to, qh, kl, start=False, stop=False, skip_group_check=True)
                    last = pe.matmul(to, ql, kh, start=False, stop=g == 1, skip_group_check=True)
                last.then_inc(s_ready, 1)

            def values_of(b):
                for h in range(2):
                    for c in range(DC):
                        last = pe.matmul(ps_m[1][64 * h:64 * (h + 1), KV * b:KV * (b + 1)], ctxT[:, c, b, :], wv[:, c, :],
                                         start=c == 0, stop=c == DC - 1)
                return last

            def probs_T(t, c):
                if c % 2 == 0:
                    pe.wait_ge(exp_done, SB * t + (2 if c == 0 else 4))
                for i in range(4):
                    p = 4 * c + i
                    last = pe.transpose(pT_bank[t][c][:, P * i:P * (i + 1)],
                                        probs[:, t % 2, p // 2, P * (p % 2):P * (p % 2 + 1)], ident[:])
                last.then_inc(pT_ready, 1)

            def denominators_T(t):
                pe.wait_ge(rden_done, t + 1)
                transposes(rT_bank[t % 2], rden_wide.rearrange("p h d -> p (h d)")).then_inc(rT_ready, 1)

            def attention(t):
                pe.wait_ge(vb_done, 2 * (t // TB + 1))
                for c in range(DC):
                    pe.wait_ge(pT_done, DC * t + c + 1)
                    for i in range(4):
                        p = 4 * c + i
                        last = pe.matmul(ps_m[0][32 * i:32 * (i + 1), P * c:P * (c + 1)],
                                         vb[:, p // 2, :, :].rearrange("p h d -> p (h d)"), pT[:, p, :],
                                         start=True, stop=True)
                last.then_inc(pv_ready, 1)

            def out_projection(t):
                pe.wait_ge(attn_lo_done, t + 1)
                if t == 0:
                    pe.wait_ge(w_split, DC)
                for c in range(DC):
                    last = split3(pe, out_bank[t][:], attn_hi[:, c, :], attn_lo[:, c, :],
                                  wo_hi[:, c, :], wo_lo[:, c, :], c == 0, c == DC - 1)
                last.then_inc(o_ready, 1)

            def tokens2_T(t):
                pe.wait_ge(xn2_ready, t + 1)
                transposes(x2T_bank[t], xn2).then_inc(x2T_ready, 1)

            def last_halves(name, src):
                for c in range(DC):
                    ins = pe.transpose(last_banks[name][c // 2][:, P * c:P * (c + 1)], src[:, P * c:P * (c + 1)], ident[:])
                    if c % 2:
                        ins.then_inc(last_ready, 1)

            def expert_columns(t, half_of):
                if t < NT - 1:
                    pe.wait_ge(x2T_lo_done, t + 1)
                if t == 0:
                    pe.wait_ge(w_split, 2 * DC)
                    pe.wait_ge(m_lo_done, 1)
                bank, cols = z_banks[t][half_of], (slice(0, ZA), slice(ZA, D + E))[half_of]
                for c in range(DC):
                    if t == NT - 1 and c % 2 == 0:
                        pe.wait_ge(last_lo_done, c // 2 + 1)
                    last = split3(pe, bank[:, 0:ZA], x2T_hi[:, c, :], x2T_lo[:, c, :],
                                  aw_hi[:, c, cols], aw_lo[:, c, cols], c == 0, c == DC - 1)
                last.then_inc((za_ready, zb_ready)[half_of], 1)

            def gated_T(t):
                pe.wait_ge(zg_done, t + 1)
                transposes(zgT_bank, zg).then_inc(zgT_ready, 1)

            def expert_output(t, of=range(DC)):
                if t < NT - 1:
                    pe.wait_ge(zgT_lo_done, t + 1)
                if t == 0:
                    pe.wait_ge(w_split, 3 * DC)
                for c in of:
                    if t == NT - 1 and c % 2 == 0:
                        pe.wait_ge(last_lo_done, c // 2 + 3)
                    last = split3(pe, y_bank[t][:], zgT_hi[:, c, :], zgT_lo[:, c, :],
                                  bw_hi[:, c, :], bw_lo[:, c, :], c == 0, c == DC - 1)
                if c == DC - 1:
                    last.then_inc(y_ready, 1)

            pe.wait_ge(consts, 1)
            for i in range(WARM_UP):
                last = pe.matmul(ps_s[2][:, 0:P], ident_bf[:], ident_bf[:], start=True, stop=True)
            pe.wait_ge(ctx_in_s, 16)
            pe.wait_ge(wk_in_s, 16)
            for c in range(DC):
                last = pe.matmul(ps_s[0][:, 0:B * CT], wk[:, c, :], ctxT[:, c, :, :].rearrange("p b s -> p (b s)"),
                                 start=c == 0, stop=c == DC - 1)
            last.then_inc(k_all_ready, 1)
            pe.wait_ge(consts, 2)
            for t in range(TB):
                tokens_T(0, t)
            pe.wait_ge(k_all_done, 1)
            for f in range(DC):
                last = pe.matmul(ps_s[1 + f // 2][:, B * CT * (f % 2):B * CT * (f % 2 + 1)], pick[:, f, :], k_all[:],
                                 start=True, stop=True)
            last.then_inc(k_ready, 1)
            for j in range(2):
                queries(0, j)
            pe.wait_ge(small_in_s, 80)
            for c in range(DC):
                last = pe.matmul(ps_m[2][:, E * c:E * (c + 1)], wr[:, P * c:P * (c + 1)], keysT[:], start=True, stop=True)
            last.then_inc(m_ready, 1)
            pe.wait_ge(wv_in_s, 16)
            values_of(0)
            pe.wait_ge(k_lo_done, 1)
            pe.wait_ge(mask_ready, 1)
            scores(0, 0)
            values_of(1)
            scores(0, 1)
            tokens_T(1, 0)
            scores(0, 2)
            values_of(2)
            scores(0, 3)
            probs_T(0, 0)
            values_of(3).then_inc(v_ready, 1)
            scores(1, 0)
            tokens_T(1, 1)
            scores(1, 1)
            scores(1, 2)
            pe.wait_ge(xT_lo_done, 2 * TB)
            probs_T(0, 1)
            queries(1, 0)
            scores(1, 3)
            pe.wait_ge(pT_done, 2)
            probs_T(0, 2)
            probs_T(0, 3)

            for b in range(B - 1):
                s = TB * b
                if s:
                    probs_T(s, 1)
                    pe.wait_ge(pT_done, DC * s + 1)
                    tokens2_T(s - 1)
                    queries(b + 1, 0)
                    pe.wait_ge(pT_done, DC * s + 2)
                    probs_T(s, 2)
                    pe.wait_ge(x2T_lo_done, s)
                    probs_T(s, 3)
                    pe.wait_ge(y_done, s - 1)
                    expert_columns(s - 1, 1)
                    expert_columns(s - 1, 0)
                pe.wait_ge(pT_done, DC * s + 3)
                denominators_T(s)
                pe.wait_ge(q_lo_done, 2 * (b + 1) + 1)
                attention(s)
                queries(b + 1, 1)
                if s:
                    pe.wait_ge(rT_done, s + 1)
                    gated_T(s - 1)
                out_projection(s)
                for j in range(SB):
                    if s == 0 and j == 3:
                        probs_T(1, 0)
                        probs_T(1, 1)
                    scores(s + 2, j)
                if s:
                    expert_output(s - 1, (0, 1))
                tokens2_T(s)
                if s:
                    expert_output(s - 1, (2, 3))

                s = TB * b + 1
                if b:
                    probs_T(s, 0)
                    pe.wait_ge(x2T_lo_done, s)
                    probs_T(s, 1)
                    expert_columns(s - 1, 0)
                    pe.wait_ge(pT_done, DC * s + 1)
                    probs_T(s, 2)
                    pe.wait_ge(pT_done, DC * s + 2)
                    probs_T(s, 3)
                else:
                    pe.wait_ge(pT_done, DC + 2)
                    probs_T(1, 2)
                    probs_T(1, 3)
                    expert_columns(0, 0)
                    pe.wait_ge(pT_done, 2 * DC)
                if b:
                    pe.wait_ge(y_done, s - 1)
                expert_columns(s - 1, 1)
                pe.wait_ge(pT_done, DC * s + 3)
                denominators_T(s)
                attention(s)
                scores(s + 2, 0)
                if b + 2 < B:
                    tokens_T(b + 2, 0)
                scores(s + 2, 1)
                if b + 2 < B:
                    pe.wait_ge(rT_done, s + 1)
                    tokens_T(b + 2, 1)
                scores(s + 2, 2)
                if b + 2 < B:
                    pe.wait_ge(xT_lo_done, TB * (b + 2) + 1)
                gated_T(s - 1)
                out_projection(s)
                expert_output(s - 1)
                if b + 2 < B:
                    pe.wait_ge(xT_lo_done, TB * (b + 3))
                probs_T(s + 1, 0)
                scores(s + 2, 3)

            t = NT - 2
            probs_T(t, 1)
            pe.wait_ge(pT_done, DC * t + 1)
            tokens2_T(t - 1)
            pe.wait_ge(sub_done, SB * NT - 1)
            probs_T(t, 2)
            probs_T(t, 3)
            pe.wait_ge(pT_done, DC * t + 2)
            denominators_T(t)
            attention(t)
            pe.wait_ge(y_done, t - 1)
            expert_columns(t - 1, 1)
            expert_columns(t - 1, 0)
            pe.wait_ge(sub_done, SB * NT)
            out_projection(t)
            probs_T(t + 1, 0)
            pe.wait_ge(rT_done, t + 1)
            probs_T(t + 1, 1)
            probs_T(t + 1, 2)
            probs_T(t + 1, 3)
            pe.wait_ge(pT_done, DC * (t + 1) + 2)
            denominators_T(t + 1)
            gated_T(t - 1)
            attention(t + 1)
            tokens2_T(t)
            expert_output(t - 1)
            out_projection(t + 1)
            pe.wait_ge(y_done, t)
            expert_columns(t, 1)
            expert_columns(t, 0)
            pe.wait_ge(xn2_ready, NT)
            last_halves("x2T", xn2)
            expert_columns(t + 1, 1)
            gated_T(t)
            expert_columns(t + 1, 0)
            expert_output(t)
            pe.wait_ge(zg_done, NT)
            last_halves("zgT", zg)
            expert_output(t + 1)


def kernel(**inputs):
    import numpy as _np
    import concourse.bacc as _bacc
    from concourse import mybir as _mybir
    from concourse.bass_utils import run_bass_kernel_spmd as _run

    i = {k: _np.asarray(a) for k, a in inputs.items()}

    def on_partitions(a):
        return a.reshape(a.shape[0] // 128, 128, *a.shape[1:]).swapaxes(0, 1)

    laid = {
        "x": i["x"],
        "ctxT": on_partitions(i["ctx_4096"].transpose(2, 0, 1)),
        "mask": i["mask_SxS2_bk0"],
        "g_attn": i["g_xattn"],
        "g_ffn": i["g_ffn"],
        "wqT": on_partitions(i["L0_xattn_w_q"].T),
        "wkT": on_partitions(i["L0_xattn_w_k"].T),
        "wvT": on_partitions(i["L0_xattn_w_v"].T),
        "woT": on_partitions(i["L0_xattn_w_out"].T),
        "aT": on_partitions(i["L0_ffn_A_w"].T),
        "bT": on_partitions(i["L0_ffn_B_w"].T),
        "wr": i["L0_ffn_Wq_w"],
        "keysT": i["L0_ffn_keys"].T,
    }
    nc = _bacc.Bacc("TRN2", target_bir_lowering=False, num_devices=1)
    arrays, args = {}, []
    for name, a in laid.items():
        a = _np.ascontiguousarray(a)
        arrays[f"in_{name}"] = a
        args.append(nc.dram_tensor(f"in_{name}", a.shape, _mybir.dt.from_np(a.dtype), kind="ExternalInput").ap())
    args.append(nc.dram_tensor("out_x", i["x"].shape, _mybir.dt.float32, kind="ExternalOutput").ap())
    gated_cross_attention_kernel(nc, *args)
    r = _run(nc, [arrays], core_ids=[0])
    return r.results[0]["out_x"]
```

```python
import concourse.bass as bass
from concourse import mybir
from contextlib import ExitStack


def gated_cross_attention_kernel(nc, x_in, ctxT_in, maskT_in, g_attn_in, g_ffn_in,
                                 wqT_in, wkT_in, wvT_in, woT_in, aT_in, bT_in, wr_in, keysT_in,
                                 out):
    f32 = mybir.dt.float32
    f32r = mybir.dt.float32r
    bf16 = mybir.dt.bfloat16
    ALU = mybir.AluOpType
    ACT = mybir.ActivationFunctionType
    AX = mybir.AxisListType

    P = 128
    B, S, D = x_in.shape
    CT = ctxT_in.shape[3]
    KV = wkT_in.shape[2]
    E = keysT_in.shape[1]
    R = wr_in.shape[0]
    H, DH = 32, 16
    G = KV // DH
    HG = H // G
    RANK = D // E
    TB = S // P
    NT = B * TB
    DC = D // P
    GW = HG * CT
    SB = 4
    ZA = 288
    ZB = D - ZA
    EA = ZA // RANK
    EPS = 1e-5
    SCALE = DH ** -0.5
    SCALING = 32 / 16
    BIG = 3.3895313892515355e38
    WARM_UP = 64
    TAKEN = -3.0e38

    ctx = ExitStack()
    with ctx:
        def sb(name, shape, dt=f32):
            return ctx.enter_context(nc.sbuf_tensor(name, shape, dt))

        def pb(name):
            return ctx.enter_context(nc.psum_tensor(name, [P, 512], f32))

        def sem(name):
            return ctx.enter_context(nc.semaphore(name))

        x = sb("x", [P, NT, D])
        wq = sb("wq", [P, DC, D])
        wo = sb("wo", [P, DC, D])
        aw = sb("aw", [P, DC, D + E])
        bw = wo
        wq_hi, wq_lo = sb("wq_hi", [P, DC, D], f32r), sb("wq_lo", [P, DC, D], f32r)
        wo_hi, wo_lo = sb("wo_hi", [P, DC, D], f32r), sb("wo_lo", [P, DC, D], f32r)
        aw_hi, aw_lo = sb("aw_hi", [P, DC, D + E], f32r), sb("aw_lo", [P, DC, D + E], f32r)
        bw_hi, bw_lo = sb("bw_hi", [P, DC, D], f32r), sb("bw_lo", [P, DC, D], f32r)
        wk = sb("wk", [P, DC, KV])
        wv = sb("wv", [P, DC, KV])
        ctxT = sb("ctxT", [P, DC, B, CT])
        maskT = sb("maskT", [P, S], maskT_in.dtype)
        gates = sb("gates", [P, 2])
        wr = sb("wr", [R, D])
        keysT = sb("keysT", [R, E])

        ident = sb("ident", [P, P])
        ident_bf = sb("ident_bf", [P, P], bf16)
        head_of_four = sb("head_of_four", [P, HG])
        half = sb("half", [P, 2])
        shift = sb("shift", [P, TB])
        neg_half = sb("neg_half", [P, TB])
        tanh_g = sb("tanh_g", [P, 2])

        k_all = sb("k_all", [P, B * CT])
        pick = sb("pick", [P, DC, P])
        k_hi, k_lo = sb("k_hi", [P, DC, B, CT], f32r), sb("k_lo", [P, DC, B, CT], f32r)
        kb_hi = sb("kb_hi", [P, DC, 2, HG, CT], f32r)
        kb_lo = sb("kb_lo", [P, DC, HG, CT], f32r)
        v = sb("v", [P, B, G, DH])
        vb = sb("vb", [P, G, 2, DH])

        stats = sb("stats", [P, TB, 6])
        mv = sb("mv", [P, TB, 2])
        veps = sb("veps", [P, TB])
        rstd = sb("rstd", [P, TB])
        xn = sb("xn", [P, TB, D])
        xT_hi, xT_lo = sb("xT_hi", [P, DC, S], f32r), sb("xT_lo", [P, DC, S], f32r)
        qT_hi, qT_lo = sb("qT_hi", [P, DC, S], f32r), sb("qT_lo", [P, DC, S], f32r)
        q_mask = sb("q_mask", [P, DC, 2, S], f32r)

        probs = sb("probs", [P, 2, G, GW])
        smax = sb("smax", [P, SB, 2 * HG])
        den = sb("den", [P, SB, 2 * HG])
        rden = sb("rden", [P, SB, 2 * HG])
        rden_wide = wk[:].rearrange("p c (a d) -> p (c a) d", d=DH)
        pT_first = sb("pT", [P, 2, 4, P])
        pT_rest = ctxT[:].rearrange("p (k c) b s -> p k (c b s)", k=2).rearrange("p k (a n) -> p k a n", n=P)
        pT = [pT_first[:, 0, :, :], pT_first[:, 1, :, :], pT_rest[:, 0, :, :], pT_rest[:, 1, :, :]]
        rdenT, attn, xn2, zg = (wq[:, c, :] for c in range(DC))
        attn_hi, attn_lo = sb("attn_hi", [P, DC, P], f32r), sb("attn_lo", [P, DC, P], f32r)

        stats2 = sb("stats2", [P, 6])
        mv2 = sb("mv2", [P, 2])
        veps2 = sb("veps2", [P, 1])
        rstd2 = sb("rstd2", [P, 1])
        x2T_hi, x2T_lo = sb("x2T_hi", [P, DC, P], f32r)[:], sb("x2T_lo", [P, DC, P], f32r)[:]
        zgT_hi, zgT_lo = sb("zgT_hi", [P, DC, P], f32r)[:], sb("zgT_lo", [P, DC, P], f32r)[:]
        logits = sb("logits", [P, 2, E])
        part = sb("part", [P, E])
        top = sb("top", [P, 2, 8])
        neg_top = sb("neg_top", [P, 1])
        e_exp = sb("e_exp", [P, 2, E])
        gate = sb("gate", [P, E])
        gate_sum = sb("gate_sum", [P, 1])
        gate_scale = sb("gate_scale", [P, 1])

        ps_s = [pb(f"ps_s{i}") for i in range(3)]
        ps_t = [pb(f"ps_t{i}") for i in range(2)]
        ps_m = [pb(f"ps_m{i}") for i in range(3)]
        score_bank = [ps_s[0], ps_s[1], ps_s[2], ps_s[0]]

        q_bank = [ps_m[0], ps_t[1]]
        pT_bank = [[ps_t[1], ps_t[0], ps_t[0], ps_t[1]], [ps_t[1], ps_t[0], ps_t[1], ps_t[0]]] * (B - 1) \
            + [[ps_t[1], ps_t[0], ps_s[1], ps_s[2]], [ps_t[1], ps_m[1], ps_s[1], ps_s[2]]]
        pT_bank[1] = [ps_t[1], ps_m[2], ps_t[1], ps_m[2]]
        rT_bank = [ps_t[0], ps_t[1]]
        x2T_bank = [ps_t[0], ps_t[1]] * (B - 1) + [ps_m[1], None]
        zgT_bank = ps_t[0]
        out_bank = [ps_m[1]] * (NT - 2) + [ps_s[0], ps_s[1]]
        z_banks = [(ps_m[1], ps_m[2])] * (NT - 2) + [(ps_m[1], ps_s[0]), (ps_m[2], ps_s[2])]
        y_bank = [ps_m[2]] * (NT - 2) + [ps_s[0], ps_s[1]]

        def xT_bank(b, t):
            return ps_t[0] if b == 1 else ps_t[t]

        last_banks = {"x2T": (ps_t[1], ps_m[0]), "zgT": (ps_t[0], ps_m[0])}

        def bank_probs(t, j):
            g0 = 4 * (j // 2) + j % 2
            return probs[:, t % 2, g0:g0 + 3:2, :]

        x_in_s = [sem(f"x_loaded{b}") for b in range(B)]
        wq_in_s = [sem(f"wq_loaded{j}") for j in range(2)]
        wo_in_s, aw_in_s, bw_in_s = (sem(n) for n in ("wo_loaded", "aw_loaded", "bw_loaded"))
        ctx_in_s, wk_in_s, wv_in_s, mask_in_s, small_in_s = (
            sem(n) for n in ("ctx_loaded", "wk_loaded", "wv_loaded", "mask_loaded", "small_loaded"))
        pool_step = sem("pool_step")
        consts = sem("consts_ready")
        tanh_ready = sem("tanh_ready")
        mask_ready, key_idents = sem("mask_ready"), sem("key_idents_ready")
        k_all_ready, k_all_done = sem("k_all_ready"), sem("k_all_done")
        wq_hi_ready, wq_lo_ready = sem("wq_hi_ready"), sem("wq_lo_ready")
        w_split = sem("w_split")
        k_ready, v_ready, m_ready = sem("k_ready"), sem("v_ready"), sem("m_ready")
        k_hi_done, k_lo_done, v_done, m_hi_done, m_lo_done = (sem(n) for n in ("k_hi_done", "k_lo_done", "v_done", "m_hi_done", "m_lo_done"))
        kb_done, kb_lo_first, vb_done = sem("kb_done"), sem("kb_lo_first_done"), sem("vb_done")
        dve_step = sem("dve_step")
        var_ready, rstd_ready = sem("var_ready"), sem("rstd_ready")
        xn_ready, xT_ready, xT_hi_done, xT_lo_done = (sem(n) for n in ("xn_ready", "xT_ready", "xT_hi_done", "xT_lo_done"))
        q_ready, q_hi_done, q_lo_done, q_mask_done = (sem(n) for n in ("q_ready", "q_hi_done", "q_lo_done", "q_mask_done"))
        s_ready, sub_done, exp_done = sem("scores_ready"), sem("sub_done"), sem("exp_done")
        rden_ready, rden_done = sem("rden_ready"), sem("rden_done")
        pT_ready, pT_done = sem("pT_ready"), sem("pT_done")
        pv_ready, rT_ready, rT_done, attn_done = (sem(n) for n in ("pv_ready", "rdenT_ready", "rdenT_done", "attn_done"))
        attn_hi_done, attn_lo_done = sem("attn_hi_done"), sem("attn_lo_done")
        o_ready = sem("o_ready")
        var2_ready, rstd2_ready, xn2_ready = sem("var2_ready"), sem("rstd2_ready"), sem("xn2_ready")
        x2T_ready, x2T_hi_done, x2T_lo_done = sem("x2T_ready"), sem("x2T_hi_done"), sem("x2T_lo_done")
        za_ready, zb_ready, top_done, e_exp_done, zg_done = sem("za_ready"), sem("zb_ready"), sem("top_done"), sem("e_exp_done"), sem("zg_done")
        zgT_ready, zgT_hi_done, zgT_lo_done = sem("zgT_ready"), sem("zgT_hi_done"), sem("zgT_lo_done")
        last_ready, last_hi_done, last_lo_done = sem("last_ready"), sem("last_hi_done"), sem("last_lo_done")
        y_ready, y_done, stored = sem("y_ready"), sem("y_done"), sem("stored")

        def split3(pe, to, lhs_hi, lhs_lo, rhs_hi, rhs_lo, first, last):
            pe.matmul(to, lhs_hi, rhs_hi, start=first, stop=False)
            pe.matmul(to, lhs_hi, rhs_lo, start=False, stop=False)
            return pe.matmul(to, lhs_lo, rhs_hi, start=False, stop=last)

        block = ctx.enter_context(nc.Block())

        @block.sync
        def _(sp):
            xv = x_in.rearrange("b (t p) d -> p (b t) d", p=P)
            ov = out.rearrange("b (t p) d -> p (b t) d", p=P)
            sp.dma_start(x[:, 0:TB, :], xv[:, 0:TB, :]).then_inc(x_in_s[0], 16)
            for j in range(2):
                sp.dma_start(wq[:, 2 * j:2 * j + 2, :], wqT_in[:, 2 * j:2 * j + 2, :]).then_inc(wq_in_s[j], 16)
            sp.dma_start(wr[:, :], wr_in).then_inc(small_in_s, 16)
            sp.dma_start(keysT[:, :], keysT_in).then_inc(small_in_s, 16)
            sp.dma_start(gates[:, 0:1], g_attn_in.partition_broadcast(P)).then_inc(small_in_s, 16)
            sp.dma_start(gates[:, 1:2], g_ffn_in.partition_broadcast(P)).then_inc(small_in_s, 16)
            sp.dma_start(x[:, TB:2 * TB, :], xv[:, TB:2 * TB, :]).then_inc(x_in_s[1], 16)
            sp.dma_start(wo[:, :, :], woT_in).then_inc(wo_in_s, 16)
            sp.dma_start(aw[:, :, 0:D], aT_in).then_inc(aw_in_s, 16)
            for b in range(2, B):
                sp.dma_start(x[:, TB * b:TB * (b + 1), :], xv[:, TB * b:TB * (b + 1), :]).then_inc(x_in_s[b], 16)
            sp.wait_ge(w_split, DC)
            sp.dma_start(bw[:, :, :], bT_in).then_inc(bw_in_s, 16)
            for t in range(NT):
                sp.wait_ge(y_done, t + 1)
                sp.dma_start(ov[:, t:t + 1, :], x[:, t:t + 1, :]).then_inc(stored, 16)
            sp.wait_ge(stored, 16 * NT)

        @block.gpsimd
        def _(pool):
            step = [0]

            def then(ins):
                step[0] += 1
                ins.then_inc(pool_step, 1)
                pool.wait_ge(pool_step, step[0])

            def signal(ins, to, value):
                ins.then_inc(to, 1)
                pool.wait_ge(to, value)

            then(pool.memset(neg_half[:], -0.5))
            then(pool.memset(ident[:], 0.0))
            then(pool.affine_select(out=ident[:], in_=ident[:], compare_op=ALU.not_equal, fill=1.0,
                                    base=0, pattern=[[-1, P]], channel_multiplier=1))
            signal(pool.tensor_copy(ident_bf[:], ident[:]), consts, 1)
            then(pool.memset(pick[:], 0.0))
            signal(pool.affine_select(out=pick[:].rearrange("p c (g h d) -> p (c g) h d", g=2, h=HG),
                                      in_=pick[:].rearrange("p c (g h d) -> p (c g) h d", g=2, h=HG),
                                      compare_op=ALU.not_equal, fill=1.0, base=0,
                                      pattern=[[-DH, G], [0, HG], [-1, DH]], channel_multiplier=1), consts, 2)

            def inv_sqrt(out_, veps_, var):
                then(pool.tensor_scalar(veps_, var, EPS, 0.0, ALU.add, ALU.add))
                return pool.tensor_tensor(out_, veps_, neg_half[:, 0:veps_.shape[1]], ALU.pow)

            def rstd_batch(b):
                pool.wait_ge(var_ready, b + 1)
                if b:
                    pool.wait_ge(xn_ready, TB * b)
                then(inv_sqrt(rstd[:], veps[:], mv[:, :, 1]))
                then(pool.tensor_tensor(shift[:], mv[:, :, 0], rstd[:], ALU.mult))
                signal(pool.tensor_scalar(shift[:], shift[:], -1.0, 0.0, ALU.mult, ALU.add), rstd_ready, b + 1)

            def split_weight(hi, lo, w, loaded, n, of=range(DC)):
                pool.wait_ge(loaded, 16)
                for c in of:
                    then(pool.tensor_scalar(hi[:, c, 0:D], w[:, c, 0:D], 1.0, 0.0, ALU.mult, ALU.add))
                    signal(pool.tensor_tensor(lo[:, c, 0:D], w[:, c, 0:D], hi[:, c, 0:D].bitcast(f32),
                                              ALU.subtract), w_split, DC * n + c + 1)

            def keys(b):
                if b:
                    pool.wait_ge(s_ready, SB * TB * b)
                for g2 in range(2):
                    rows = slice(CT * g2, CT * (g2 + 1))
                    for hh in range(HG):
                        signal(pool.tensor_scalar(kb_hi[rows, :, g2, hh, :], k_hi[rows, :, b, :].bitcast(f32),
                                                  head_of_four[rows, hh:hh + 1], 0.0, ALU.mult, ALU.add),
                               kb_done, HG * (3 * b + g2 - (1 if b else 0)) + hh + 1)
                for hh in range(HG if b else 0):
                    signal(pool.tensor_scalar(kb_lo[:, :, hh, :], k_lo[:, :, b, :].bitcast(f32),
                                              head_of_four[:, hh:hh + 1], 0.0, ALU.mult, ALU.add),
                           kb_done, HG * (3 * b + 1) + hh + 1)

            def values(b):
                if b:
                    pool.wait_ge(pv_ready, TB * b)
                for h in range(2):
                    signal(pool.tensor_scalar(vb[:, :, h, :], v[:, b, :, :], half[:, h:h + 1], 0.0,
                                              ALU.mult, ALU.add), vb_done, 2 * b + h + 1)

            rstd_batch(0)
            then(pool.memset(half[:], 1.0))
            then(pool.affine_select(out=half[:], in_=half[:], compare_op=ALU.is_ge, fill=0.0,
                                    base=0, pattern=[[-CT, 2]], channel_multiplier=1))
            signal(pool.affine_select(out=half[:], in_=half[:], compare_op=ALU.is_ge, fill=0.0,
                                      base=CT - 1, pattern=[[CT, 2]], channel_multiplier=-1), consts, 3)
            then(pool.memset(head_of_four[:], SCALE))
            for g2 in range(2):
                rows = head_of_four[64 * g2:64 * (g2 + 1), :]
                then(pool.affine_select(out=rows, in_=rows, compare_op=ALU.is_ge, fill=0.0,
                                        base=0, pattern=[[-DH, HG]], channel_multiplier=1))
                signal(pool.affine_select(out=rows, in_=rows, compare_op=ALU.is_ge, fill=0.0,
                                          base=DH - 1, pattern=[[DH, HG]], channel_multiplier=-1), consts, 4 + g2)

            for g2 in range(2):
                rows = slice(CT * (1 - g2), CT * (2 - g2))
                signal(pool.tensor_scalar(kb_hi[rows, :, g2, :, :], ident[rows, rows].unsqueeze(1).unsqueeze(1)
                                          .to_broadcast([CT, DC, HG, CT]), 1.0, 0.0, ALU.mult, ALU.add), key_idents, g2 + 1)
            pool.wait_ge(k_hi_done, 2)
            keys(0)
            rstd_batch(1)
            split_weight(wo_hi, wo_lo, wo, wo_in_s, 0)
            pool.wait_ge(v_done, 1)
            values(0)
            split_weight(aw_hi, aw_lo, aw, aw_in_s, 1, range(3))
            keys(1)
            split_weight(aw_hi, aw_lo, aw, aw_in_s, 1, range(3, DC))
            for s in range(NT):
                b = s // TB
                if s and s % TB == 0 and b + 1 < B:
                    keys(b + 1)
                if s % TB == 1 and b + 1 < B:
                    values(b + 1)
                if s % TB == 0 and b + 2 < B:
                    rstd_batch(b + 2)
                pool.wait_ge(var2_ready, s + 1)
                signal(inv_sqrt(rstd2[:], veps2[:], mv2[:, 1:2]), rstd2_ready, s + 1)
                if s == 0:
                    split_weight(bw_hi, bw_lo, bw, bw_in_s, 2)

        @block.scalar
        def _(act):
            act.dma_start(ctxT[:, :, :, :], ctxT_in).then_inc(ctx_in_s, 16)
            act.dma_start(wk[:, :, :], wkT_in).then_inc(wk_in_s, 16)
            for h in range(2):
                act.dma_start(maskT[CT * h:CT * (h + 1), :], maskT_in).then_inc(mask_in_s, 16)
            act.dma_start(wv[:, :, :], wvT_in).then_inc(wv_in_s, 16)

            def copy_hi(to, src, done):
                act.copy(to, src).then_inc(done, 1)

            def flat(a):
                return a.rearrange("p c n -> p (c n)")

            def normalise(b):
                act.wait_ge(rstd_ready, b + 1)
                if b:
                    act.wait_ge(xT_ready, TB * b)
                for t in range(TB):
                    act.activation(xn[:, t, :], x[:, TB * b + t, :], ACT.Identity, scale=rstd[:, t:t + 1],
                                   bias=shift[:, t:t + 1]).then_inc(xn_ready, 1)

            def tokens_T(b, t):
                act.wait_ge(xT_ready, TB * b + t + 1)
                copy_hi(xT_hi[:, :, P * t:P * (t + 1)], xT_bank(b, t)[:].rearrange("p (c n) -> p c n", c=DC), xT_hi_done)

            def queries(b, j):
                act.wait_ge(q_ready, 2 * b + j + 1)
                if b:
                    act.wait_ge(s_ready, SB * TB * b)
                copy_hi(qT_hi[:, 2 * j:2 * j + 2, :], q_bank[j][:].rearrange("p (c n) -> p c n", c=2), q_hi_done)

            def queries_beside_mask(b, j):
                act.wait_ge(q_hi_done, 2 * b + j + 1)
                for g2 in range(2):
                    rows = slice(CT * g2, CT * (g2 + 1))
                    act.copy(q_mask[rows, 2 * j:2 * j + 2, g2, :], qT_hi[rows, 2 * j:2 * j + 2, :]).then_inc(q_mask_done, 1)

            def exps(t, j):
                act.wait_ge(sub_done, SB * t + j + 1)
                view = bank_probs(t, j)
                act.activation(view, view, ACT.Exp).then_inc(exp_done, 1)

            def probs_T(t, c):
                act.wait_ge(pT_ready, DC * t + c + 1)
                if t and c == 0:
                    act.wait_ge(pv_ready, t)
                act.copy(pT[c].rearrange("p a n -> p (a n)"), pT_bank[t][c][:]).then_inc(pT_done, 1)

            def denominators(t):
                act.wait_ge(rden_ready, t + 1)
                if t:
                    act.wait_ge(rT_ready, t)
                act.copy(rden_wide, rden[:].rearrange("p j h -> p (j h)").unsqueeze(2)
                         .to_broadcast([P, H, DH])).then_inc(rden_done, 1)

            def attention(t):
                act.wait_ge(rT_ready, t + 1)
                if t:
                    act.wait_ge(attn_done, t)
                act.copy(rdenT, rT_bank[t % 2][:]).then_inc(rT_done, 1)

            def attention_hi(t):
                act.wait_ge(attn_done, t + 1)
                if t:
                    act.wait_ge(o_ready, t)
                act.copy(flat(attn_hi[:]), attn).then_inc(attn_hi_done, 1)

            def router(t):
                act.wait_ge(top_done, t + 1)
                act.activation(e_exp[:], logits[:], ACT.Exp, bias=neg_top[:]).then_inc(e_exp_done, 1)

            def gated_T(t):
                act.wait_ge(zgT_ready, t + 1)
                if t:
                    act.wait_ge(y_ready, t)
                copy_hi(flat(zgT_hi), zgT_bank[:], zgT_hi_done)

            def tokens2_T(t):
                act.wait_ge(x2T_ready, t + 1)
                if t:
                    act.wait_ge(za_ready, t)
                    act.wait_ge(zb_ready, t)
                copy_hi(flat(x2T_hi), x2T_bank[t][:], x2T_hi_done)

            def split_wq(j):
                act.wait_ge(wq_in_s[j], 16)
                for c in range(2 * j, 2 * j + 2):
                    copy_hi(wq_hi[:, c, :], wq[:, c, :], wq_hi_ready)

            def last_half(name, hi, h, n):
                act.wait_ge(last_ready, n)
                half_of = slice(2 * P * h, 2 * P * (h + 1))
                copy_hi(flat(hi)[:, half_of], last_banks[name][h][:, half_of], last_hi_done)

            normalise(0)
            split_wq(0)
            split_wq(1)
            act.wait_ge(k_all_ready, 1)
            act.copy(k_all[:], ps_s[0][:, 0:B * CT]).then_inc(k_all_done, 1)
            tokens_T(0, 0)
            tokens_T(0, 1)
            act.wait_ge(k_ready, 1)
            for j in range(2):
                copy_hi(k_hi[:, 2 * j:2 * j + 2, :, :].rearrange("p c b s -> p (c b s)"), ps_s[1 + j][:], k_hi_done)
            act.wait_ge(k_lo_done, 1)
            act.wait_ge(consts, 5)
            for hh in range(HG):
                act.activation(kb_lo[:, :, hh, :], k_lo[:, :, 0, :].bitcast(f32), ACT.Identity,
                               scale=head_of_four[:, hh:hh + 1]).then_inc(kb_lo_first, 1)
            for j in range(2):
                queries(0, j)
                queries_beside_mask(0, j)
            act.wait_ge(small_in_s, 64)
            act.activation(tanh_g[:], gates[:], ACT.Tanh).then_inc(tanh_ready, 1)
            act.wait_ge(m_ready, 1)
            copy_hi(aw_hi[:, :, D:D + E], ps_m[2][:, 0:DC * E].rearrange("p (c e) -> p c e", c=DC), m_hi_done)
            normalise(1)
            exps(0, 0)
            exps(0, 1)
            tokens_T(1, 0)
            exps(0, 2)
            probs_T(0, 0)
            exps(0, 3)
            act.wait_ge(v_ready, 1)
            act.copy(v[:].rearrange("p b g d -> p (b g d)"), ps_m[1][:]).then_inc(v_done, 1)
            tokens_T(1, 1)
            probs_T(0, 1)
            exps(1, 0)
            exps(1, 1)
            denominators(0)
            queries(1, 0)
            probs_T(0, 2)
            exps(1, 2)
            probs_T(0, 3)

            for s in range(NT - TB):
                b = s // TB
                if s > 1:
                    probs_T(s, 0)
                    probs_T(s, 1)
                if s and s % TB == 0:
                    exps(s + 1, 2)
                    tokens2_T(s - 1)
                    exps(s + 1, 3)
                    queries(b + 1, 0)
                if s % TB:
                    exps(s + 1, 3)
                if s > 1:
                    probs_T(s, 2)
                    probs_T(s, 3)
                if s > 1:
                    denominators(s)
                if s and s % TB == 0:
                    queries_beside_mask(b + 1, 0)
                attention(s)
                if s == 0:
                    exps(1, 3)
                if s:
                    router(s - 1)
                if s % TB and b + 2 < B:
                    tokens_T(b + 2, 0)
                attention_hi(s)
                if s == 0:
                    queries_beside_mask(1, 0)
                    queries(1, 1)
                    queries_beside_mask(1, 1)
                    probs_T(1, 0)
                    exps(2, 0)
                    probs_T(1, 1)
                    tokens2_T(0)
                    exps(2, 1)
                    probs_T(1, 2)
                    probs_T(1, 3)
                    normalise(2)
                    denominators(1)
                    exps(2, 2)
                elif s % TB == 0:
                    queries(b + 1, 1)
                    gated_T(s - 1)
                    queries_beside_mask(b + 1, 1)
                    if b + 2 < B:
                        normalise(b + 2)
                    exps(s + 2, 0)
                    exps(s + 2, 1)
                    tokens2_T(s)
                    exps(s + 2, 2)
                else:
                    if b + 2 < B:
                        tokens_T(b + 2, 1)
                    gated_T(s - 1)
                    exps(s + 2, 0)
                    exps(s + 2, 1)

            t = NT - 2
            probs_T(t, 0)
            probs_T(t, 1)
            tokens2_T(t - 1)
            probs_T(t, 2)
            probs_T(t, 3)
            exps(t + 1, 2)
            exps(t + 1, 3)
            denominators(t)
            router(t - 1)
            attention(t)
            probs_T(t + 1, 0)
            attention_hi(t)
            gated_T(t - 1)
            for c in range(1, DC):
                probs_T(t + 1, c)
            denominators(t + 1)
            attention(t + 1)
            attention_hi(t + 1)
            tokens2_T(t)
            act.wait_ge(za_ready, t + 1)
            act.wait_ge(zb_ready, t + 1)
            for h in range(2):
                last_half("x2T", x2T_hi, h, h + 1)
            router(t)
            gated_T(t)
            router(t + 1)
            act.wait_ge(za_ready, t + 2)
            act.wait_ge(zb_ready, t + 2)
            for h in range(2):
                last_half("zgT", x2T_hi, h, h + 3)

        @block.vector
        def _(dve):
            step = [0]

            def then(ins):
                step[0] += 1
                ins.then_inc(dve_step, 1)
                dve.wait_ge(dve_step, step[0])

            def low(to, whole, hi):
                return dve.tensor_tensor(to, whole, hi.bitcast(f32), ALU.subtract)

            def flat(a):
                return a.rearrange("p c n -> p (c n)")

            stats_step = [0]

            def tile_stats(b, t):
                dve.wait_ge(x_in_s[b], 16)
                dve.bn_stats(stats[:, t, :], x[:, TB * b + t, :]).then_inc(dve_step, 1)
                step[0] += 1
                stats_step[0] = step[0]

            def batch_variance(b):
                if b:
                    dve.wait_ge(rstd_ready, b)
                dve.wait_ge(dve_step, stats_step[0])
                for t in range(TB):
                    ins = dve.bn_aggr(mv[:, t, :], stats[:, t, :])
                ins.then_inc(var_ready, 1)

            def tokens_T(b, t):
                dve.wait_ge(xT_hi_done, TB * b + t + 1)
                low(xT_lo[:, :, P * t:P * (t + 1)], xT_bank(b, t)[:].rearrange("p (c n) -> p c n", c=DC),
                    xT_hi[:, :, P * t:P * (t + 1)]).then_inc(xT_lo_done, 1)

            def queries(b, j):
                dve.wait_ge(q_hi_done, 2 * b + j + 1)
                low(qT_lo[:, 2 * j:2 * j + 2, :], q_bank[j][:].rearrange("p (c n) -> p c n", c=2),
                    qT_hi[:, 2 * j:2 * j + 2, :]).then_inc(q_lo_done, 1)

            max_step, scale_step, x2_step = {}, [0], [0]

            def row_max(t, j):
                dve.wait_ge(s_ready, SB * t + j + 1)
                dve.reduce_max(smax[:, j, :], score_bank[j][:].rearrange("p (h s) -> p h s", s=CT), AX.X) \
                    .then_inc(dve_step, 1)
                step[0] += 1
                max_step[j] = step[0]

            def take_off(t, j):
                dve.wait_ge(dve_step, max_step[j])
                if t >= 2 and j == 0:
                    dve.wait_ge(pT_ready, DC * (t - 1))
                dve.tensor_tensor(bank_probs(t, j).rearrange("p g (h s) -> p g h s", s=CT),
                                  score_bank[j][:].rearrange("p (g h s) -> p g h s", g=2, s=CT),
                                  smax[:, j, :].rearrange("p (g h) -> p g h", g=2).unsqueeze(3)
                                  .to_broadcast([P, 2, HG, CT]), ALU.subtract).then_inc(sub_done, 1)

            def softmax_sums(t, j):
                if t and j == 0:
                    dve.wait_ge(rden_done, t)
                dve.wait_ge(exp_done, SB * t + j + 1)
                ins = dve.reduce_sum(den[:, 2 * (j // 2):2 * (j // 2) + 2, (j % 2) * HG:(j % 2 + 1) * HG],
                                     bank_probs(t, j).rearrange("p g (h s) -> p g h s", s=CT), AX.X)
                if j == SB - 1:
                    then(ins)
                    dve.reciprocal(rden[:], den[:]).then_inc(rden_ready, 1)

            def attention(t):
                dve.wait_ge(pv_ready, t + 1)
                dve.wait_ge(rT_done, t + 1)
                if t:
                    dve.wait_ge(attn_hi_done, t)
                dve.tensor_tensor(attn, ps_m[0][:], rdenT, ALU.mult).then_inc(attn_done, 1)

            def attention_lo(t):
                dve.wait_ge(attn_hi_done, t + 1)
                low(flat(attn_lo[:]), attn, flat(attn_hi[:])).then_inc(attn_lo_done, 1)

            def router(t):
                dve.wait_ge(zb_ready, t + 1)
                then(dve.tensor_copy(logits[:, 0, :], z_banks[t][1][:, ZB:ZB + E]))
                then(dve.max(top[:, 0, :], logits[:, 0, :]))
                then(dve.match_replace(part[:], top[:, 0, :], logits[:, 0, :], TAKEN))
                then(dve.max(top[:, 1, :], part[:]))
                dve.tensor_scalar(neg_top[:], top[:, 0, 0:1], -1.0, None, ALU.mult)
                dve.match_replace(logits[:, 1, :], top[:, 1, :], part[:], TAKEN).then_inc(top_done, 1)

            def gating(t):
                dve.wait_ge(e_exp_done, t + 1)
                then(dve.tensor_tensor(gate[:], e_exp[:, 0, :], e_exp[:, 1, :], ALU.subtract))
                dve.wait_ge(za_ready, t + 1)
                if t:
                    dve.wait_ge(zgT_ready, t)
                dve.tensor_tensor(zg[:, 0:ZA].rearrange("p (e r) -> p e r", r=RANK),
                                  z_banks[t][0][:, 0:ZA].rearrange("p (e r) -> p e r", r=RANK),
                                  gate[:, 0:EA].unsqueeze(2).to_broadcast([P, EA, RANK]), ALU.mult)
                dve.tensor_tensor(zg[:, ZA:D].rearrange("p (e r) -> p e r", r=RANK),
                                  z_banks[t][1][:, 0:ZB].rearrange("p (e r) -> p e r", r=RANK),
                                  gate[:, EA:E].unsqueeze(2).to_broadcast([P, E - EA, RANK]), ALU.mult) \
                    .then_inc(zg_done, 1)

            def gate_sums(t):
                then(dve.reduce_sum(gate_sum[:], gate[:], AX.X))
                then(dve.reciprocal(gate_sum[:], gate_sum[:]))
                dve.tensor_scalar(gate_scale[:], gate_sum[:], tanh_g[:, 1:2], SCALING, ALU.mult, ALU.mult) \
                    .then_inc(dve_step, 1)
                step[0] += 1
                scale_step[0] = step[0]

            def gated_T(t):
                dve.wait_ge(zgT_hi_done, t + 1)
                low(flat(zgT_lo), zgT_bank[:], flat(zgT_hi)).then_inc(zgT_lo_done, 1)

            def residual(t):
                dve.wait_ge(o_ready, t + 1)
                dve.scalar_tensor_tensor(x[:, t, :], out_bank[t][:], tanh_g[:, 0:1], x[:, t, :], ALU.mult, ALU.add) \
                    .then_inc(dve_step, 1)
                step[0] += 1
                x2_step[0] = step[0]

            def stats_of_residual(t):
                dve.wait_ge(dve_step, x2_step[0])
                then(dve.bn_stats(stats2[:], x[:, t, :]))
                dve.bn_aggr(mv2[:], stats2[:]).then_inc(var2_ready, 1)

            def normalise2(t):
                dve.wait_ge(rstd2_ready, t + 1)
                if t:
                    dve.wait_ge(x2T_ready, t)
                dve.tensor_scalar(xn2, x[:, t, :], mv2[:, 0:1], rstd2[:], ALU.subtract, ALU.mult) \
                    .then_inc(xn2_ready, 1)

            def tokens2_T(t):
                dve.wait_ge(x2T_hi_done, t + 1)
                low(flat(x2T_lo), x2T_bank[t][:], flat(x2T_hi)).then_inc(x2T_lo_done, 1)

            def result(t):
                dve.wait_ge(y_ready, t + 1)
                dve.wait_ge(dve_step, scale_step[0])
                dve.scalar_tensor_tensor(x[:, t, :], y_bank[t][:], gate_scale[:], x[:, t, :],
                                         ALU.mult, ALU.add).then_inc(y_done, 1)

            def last_half(name, hi, lo, h, n):
                dve.wait_ge(last_hi_done, n)
                half_of = slice(2 * P * h, 2 * P * (h + 1))
                low(flat(lo)[:, half_of], last_banks[name][h][:, half_of], flat(hi)[:, half_of]) \
                    .then_inc(last_lo_done, 1)

            for t in range(TB):
                tile_stats(0, t)
            batch_variance(0)
            for c in range(DC):
                dve.wait_ge(wq_hi_ready, c + 1)
                low(wq_lo[:, c, :], wq[:, c, :], wq_hi[:, c, :]).then_inc(wq_lo_ready, 1)
            tokens_T(0, 0)
            tokens_T(0, 1)
            for j in range(2):
                dve.wait_ge(k_hi_done, j + 1)
                ins = low(k_lo[:, 2 * j:2 * j + 2, :, :].rearrange("p c b s -> p (c b s)"), ps_s[1 + j][:],
                          k_hi[:, 2 * j:2 * j + 2, :, :].rearrange("p c b s -> p (c b s)"))
            ins.then_inc(k_lo_done, 1)
            dve.wait_ge(mask_in_s, 32)
            for g2 in range(2):
                rows = slice(CT * (1 - g2), CT * (2 - g2))
                dve.tensor_scalar(q_mask[rows, :, g2, :], maskT[rows, :].unsqueeze(1).to_broadcast([CT, DC, S]),
                                  1.0, BIG, ALU.subtract, ALU.mult).then_inc(mask_ready, 1)
            for t in range(TB):
                tile_stats(1, t)
            batch_variance(1)
            for j in range(2):
                queries(0, j)
            dve.wait_ge(tanh_ready, 1)
            dve.wait_ge(m_hi_done, 1)
            low(aw_lo[:, :, D:D + E], ps_m[2][:, 0:DC * E].rearrange("p (c e) -> p c e", c=DC),
                aw_hi[:, :, D:D + E]).then_inc(m_lo_done, 1)
            for j in range(SB):
                row_max(0, j)
                take_off(0, j)
                if j == 2:
                    tokens_T(1, 0)
            softmax_sums(0, 0)
            softmax_sums(0, 1)
            for j in range(SB):
                row_max(1, j)
                take_off(1, j)
                if j == 0:
                    tokens_T(1, 1)
                    softmax_sums(0, 2)
                if j == 1:
                    softmax_sums(0, 3)
                if j == 2:
                    queries(1, 0)

            for s in range(NT - TB):
                b = s // TB
                if s and s % TB == 0:
                    tokens2_T(s - 1)
                    for j in range(SB):
                        softmax_sums(s, j)
                    queries(b + 1, 0)
                    softmax_sums(s + 1, 0)
                    softmax_sums(s + 1, 1)
                elif s == NT - TB - 1:
                    softmax_sums(s + 1, 0)
                if s:
                    router(s - 1)
                attention(s)
                if s:
                    gating(s - 1)
                if s % TB and b + 2 < B:
                    tokens_T(b + 2, 0)
                attention_lo(s)
                if s == 0:
                    softmax_sums(1, 0)
                    tile_stats(2, 0)
                    queries(1, 1)
                    tile_stats(2, 1)
                    batch_variance(2)
                elif s % TB == 0:
                    gate_sums(s - 1)
                    if b + 2 < B:
                        tile_stats(b + 2, 0)
                    queries(b + 1, 1)
                    gated_T(s - 1)
                    if b + 2 < B:
                        tile_stats(b + 2, 1)
                        batch_variance(b + 2)
                if s % TB == 0:
                    residual(s)
                    if s == 0:
                        stats_of_residual(s)
                    row_max(s + 2, 0)
                    take_off(s + 2, 0)
                    if s:
                        stats_of_residual(s)
                    else:
                        normalise2(s)
                    row_max(s + 2, 1)
                    if s:
                        normalise2(s)
                    take_off(s + 2, 1)
                    if s == 0:
                        tokens2_T(s)
                        softmax_sums(1, 1)
                        softmax_sums(1, 2)
                        softmax_sums(1, 3)
                    row_max(s + 2, 2)
                    take_off(s + 2, 2)
                    if s:
                        tokens2_T(s)
                    row_max(s + 2, 3)
                    take_off(s + 2, 3)
                    if s:
                        result(s - 1)
                        softmax_sums(s + 1, 2)
                        softmax_sums(s + 1, 3)
                else:
                    if b + 2 < B:
                        tokens_T(b + 2, 1)
                    gate_sums(s - 1)
                    row_max(s + 2, 0)
                    gated_T(s - 1)
                    take_off(s + 2, 0)
                    if s == NT - TB - 1:
                        softmax_sums(s + 1, 1)
                    row_max(s + 2, 1)
                    residual(s)
                    stats_of_residual(s)
                    take_off(s + 2, 1)
                    row_max(s + 2, 2)
                    normalise2(s)
                    take_off(s + 2, 2)
                    result(s - 1)
                    if s < NT - TB - 1:
                        row_max(s + 2, 3)
                        take_off(s + 2, 3)

            t = NT - 2
            softmax_sums(t, 2)
            tokens2_T(t - 1)
            row_max(t + 1, 3)
            take_off(t + 1, 3)
            softmax_sums(t, 3)
            router(t - 1)
            softmax_sums(t + 1, 0)
            gating(t - 1)
            attention(t)
            softmax_sums(t + 1, 1)
            attention_lo(t)
            gated_T(t - 1)
            softmax_sums(t + 1, 2)
            softmax_sums(t + 1, 3)
            gate_sums(t - 1)
            residual(t)
            stats_of_residual(t)
            attention(t + 1)
            normalise2(t)
            attention_lo(t + 1)
            tokens2_T(t)
            residual(t + 1)
            stats_of_residual(t + 1)
            result(t - 1)
            normalise2(t + 1)
            router(t)
            for h in range(2):
                last_half("x2T", x2T_hi, x2T_lo, h, h + 1)
            gating(t)
            gate_sums(t)
            router(t + 1)
            gated_T(t)
            gating(t + 1)
            for h in range(2):
                last_half("zgT", x2T_hi, x2T_lo, h, h + 3)
            result(t)
            gate_sums(t + 1)
            result(t + 1)

        @block.tensor
        def _(pe):
            def transposes(bank, src):
                for c in range(DC):
                    last = pe.transpose(bank[:, P * c:P * (c + 1)], src[:, P * c:P * (c + 1)], ident[:])
                return last

            def tokens_T(b, t):
                pe.wait_ge(xn_ready, TB * b + t + 1)
                if b == 1 and t:
                    pe.wait_ge(xT_lo_done, TB * b + t)
                transposes(xT_bank(b, t), xn[:, t, :]).then_inc(xT_ready, 1)

            def queries(b, j):
                pe.wait_ge(xT_lo_done, TB * (b + 1))
                for i in range(2):
                    f = 2 * j + i
                    for c in range(DC):
                        if b == 0 and j == 0 and i == 0:
                            pe.wait_ge(wq_lo_ready, c + 1)
                        last = split3(pe, q_bank[j][:, S * i:S * (i + 1)],
                                      wq_hi[:, c, P * f:P * (f + 1)], wq_lo[:, c, P * f:P * (f + 1)],
                                      xT_hi[:, c, :], xT_lo[:, c, :], c == 0, c == DC - 1)
                last.then_inc(q_ready, 1)

            def scores(t, j):
                b, h = divmod(t, TB)
                if h == 0 and j == 0:
                    pe.wait_ge(q_lo_done, 2 * (b + 1))
                    pe.wait_ge(q_mask_done, 4 * (b + 1))
                    pe.wait_ge(kb_done, 3 * HG * b + 2 * HG)
                    pe.wait_ge(kb_lo_first, HG)
                cols = slice(P * h, P * (h + 1))
                if j == 3:
                    pe.wait_ge(sub_done, SB * t + 1)
                elif t:
                    pe.wait_ge(sub_done, SB * (t - 1) + (4 if j == 0 else j + 1))
                bank = score_bank[j]
                g2 = j % 2
                rows = slice(CT * g2, CT * (g2 + 1))
                for g in range(2):
                    c = 2 * (j // 2) + g
                    to = bank[:, GW * g:GW * (g + 1)]
                    qh, ql = qT_hi[rows, c, cols], qT_lo[rows, c, cols]
                    kh, kl = (k.rearrange("p h s -> p (h s)") for k in (kb_hi[:, c, g2, :, :], kb_lo[rows, c, :, :]))
                    pe.matmul(to, q_mask[:, c, g2, cols], kh, start=True, stop=False)
                    pe.matmul(to, qh, kl, start=False, stop=False)
                    last = pe.matmul(to, ql, kh[rows, :], start=False, stop=True)
                last.then_inc(s_ready, 1)

            def values_of(b):
                for h in range(2):
                    for c in range(DC):
                        last = pe.matmul(ps_m[1][64 * h:64 * (h + 1), KV * b:KV * (b + 1)], ctxT[:, c, b, :], wv[:, c, :],
                                         start=c == 0, stop=c == DC - 1)
                return last

            def probs_T(t, c):
                if c % 2 == 0:
                    pe.wait_ge(exp_done, SB * t + (2 if c == 0 else 4))
                for i in range(4):
                    p = 4 * c + i
                    last = pe.transpose(pT_bank[t][c][:, P * i:P * (i + 1)],
                                        probs[:, t % 2, p // 2, P * (p % 2):P * (p % 2 + 1)], ident[:])
                last.then_inc(pT_ready, 1)

            def denominators_T(t):
                pe.wait_ge(rden_done, t + 1)
                transposes(rT_bank[t % 2], rden_wide.rearrange("p h d -> p (h d)")).then_inc(rT_ready, 1)

            def attention(t):
                pe.wait_ge(vb_done, 2 * (t // TB + 1))
                for c in range(DC):
                    pe.wait_ge(pT_done, DC * t + c + 1)
                    for i in range(4):
                        p = 4 * c + i
                        last = pe.matmul(ps_m[0][32 * i:32 * (i + 1), P * c:P * (c + 1)],
                                         vb[:, p // 2, :, :].rearrange("p h d -> p (h d)"), pT[c][:, i, :],
                                         start=True, stop=True)
                last.then_inc(pv_ready, 1)

            def out_projection(t):
                pe.wait_ge(attn_lo_done, t + 1)
                if t == 0:
                    pe.wait_ge(w_split, DC)
                for c in range(DC):
                    last = split3(pe, out_bank[t][:], attn_hi[:, c, :], attn_lo[:, c, :],
                                  wo_hi[:, c, :], wo_lo[:, c, :], c == 0, c == DC - 1)
                last.then_inc(o_ready, 1)

            def tokens2_T(t):
                pe.wait_ge(xn2_ready, t + 1)
                transposes(x2T_bank[t], xn2).then_inc(x2T_ready, 1)

            def last_halves(name, src):
                for c in range(DC):
                    ins = pe.transpose(last_banks[name][c // 2][:, P * c:P * (c + 1)], src[:, P * c:P * (c + 1)], ident[:])
                    if c % 2:
                        ins.then_inc(last_ready, 1)

            def expert_columns(t, half_of):
                if t < NT - 1:
                    pe.wait_ge(x2T_lo_done, t + 1)
                if t == 0:
                    pe.wait_ge(w_split, 2 * DC)
                    pe.wait_ge(m_lo_done, 1)
                bank, cols = z_banks[t][half_of], (slice(0, ZA), slice(ZA, D + E))[half_of]
                for c in range(DC):
                    if t == NT - 1 and c % 2 == 0:
                        pe.wait_ge(last_lo_done, c // 2 + 1)
                    last = split3(pe, bank[:, 0:ZA], x2T_hi[:, c, :], x2T_lo[:, c, :],
                                  aw_hi[:, c, cols], aw_lo[:, c, cols], c == 0, c == DC - 1)
                last.then_inc((za_ready, zb_ready)[half_of], 1)

            def gated_T(t):
                pe.wait_ge(zg_done, t + 1)
                transposes(zgT_bank, zg).then_inc(zgT_ready, 1)

            def expert_output(t, of=range(DC)):
                if t < NT - 1:
                    pe.wait_ge(zgT_lo_done, t + 1)
                if t == 0:
                    pe.wait_ge(w_split, 3 * DC)
                zT_hi, zT_lo = (zgT_hi, zgT_lo) if t < NT - 1 else (x2T_hi, x2T_lo)
                for c in of:
                    if t == NT - 1 and c % 2 == 0:
                        pe.wait_ge(last_lo_done, c // 2 + 3)
                    last = split3(pe, y_bank[t][:], zT_hi[:, c, :], zT_lo[:, c, :],
                                  bw_hi[:, c, :], bw_lo[:, c, :], c == 0, c == DC - 1)
                if c == DC - 1:
                    last.then_inc(y_ready, 1)

            pe.wait_ge(consts, 1)
            for i in range(WARM_UP):
                last = pe.matmul(ps_s[2][:, 0:P], ident_bf[:], ident_bf[:], start=True, stop=True)
            pe.wait_ge(ctx_in_s, 16)
            pe.wait_ge(wk_in_s, 16)
            for c in range(DC):
                last = pe.matmul(ps_s[0][:, 0:B * CT], wk[:, c, :], ctxT[:, c, :, :].rearrange("p b s -> p (b s)"),
                                 start=c == 0, stop=c == DC - 1)
            last.then_inc(k_all_ready, 1)
            pe.wait_ge(consts, 2)
            for t in range(TB):
                tokens_T(0, t)
            pe.wait_ge(k_all_done, 1)
            for f in range(DC):
                last = pe.matmul(ps_s[1 + f // 2][:, B * CT * (f % 2):B * CT * (f % 2 + 1)], pick[:, f, :], k_all[:],
                                 start=True, stop=True)
            last.then_inc(k_ready, 1)
            for j in range(2):
                queries(0, j)
            pe.wait_ge(small_in_s, 64)
            for c in range(DC):
                last = pe.matmul(ps_m[2][:, E * c:E * (c + 1)], wr[:, P * c:P * (c + 1)], keysT[:], start=True, stop=True)
            last.then_inc(m_ready, 1)
            pe.wait_ge(wv_in_s, 16)
            values_of(0)
            pe.wait_ge(k_lo_done, 1)
            pe.wait_ge(mask_ready, 2)
            pe.wait_ge(key_idents, 2)
            scores(0, 0)
            values_of(1)
            scores(0, 1)
            tokens_T(1, 0)
            scores(0, 2)
            values_of(2)
            scores(0, 3)
            probs_T(0, 0)
            values_of(3).then_inc(v_ready, 1)
            scores(1, 0)
            tokens_T(1, 1)
            scores(1, 1)
            scores(1, 2)
            pe.wait_ge(xT_lo_done, 2 * TB)
            probs_T(0, 1)
            queries(1, 0)
            scores(1, 3)
            pe.wait_ge(pT_done, 2)
            probs_T(0, 2)
            probs_T(0, 3)

            for b in range(B - 1):
                s = TB * b
                if s:
                    probs_T(s, 1)
                    pe.wait_ge(pT_done, DC * s + 1)
                    tokens2_T(s - 1)
                    queries(b + 1, 0)
                    pe.wait_ge(pT_done, DC * s + 2)
                    probs_T(s, 2)
                    pe.wait_ge(x2T_lo_done, s)
                    probs_T(s, 3)
                    pe.wait_ge(y_done, s - 1)
                    expert_columns(s - 1, 1)
                    expert_columns(s - 1, 0)
                pe.wait_ge(pT_done, DC * s + 3)
                denominators_T(s)
                pe.wait_ge(q_lo_done, 2 * (b + 1) + 1)
                attention(s)
                queries(b + 1, 1)
                if s:
                    pe.wait_ge(rT_done, s + 1)
                    gated_T(s - 1)
                out_projection(s)
                for j in range(SB):
                    if s == 0 and j == 3:
                        probs_T(1, 0)
                        probs_T(1, 1)
                    scores(s + 2, j)
                if s:
                    expert_output(s - 1, (0, 1))
                tokens2_T(s)
                if s:
                    expert_output(s - 1, (2, 3))

                s = TB * b + 1
                if b:
                    probs_T(s, 0)
                    pe.wait_ge(x2T_lo_done, s)
                    probs_T(s, 1)
                    expert_columns(s - 1, 0)
                    pe.wait_ge(pT_done, DC * s + 1)
                    probs_T(s, 2)
                    pe.wait_ge(pT_done, DC * s + 2)
                    probs_T(s, 3)
                else:
                    pe.wait_ge(pT_done, DC + 2)
                    probs_T(1, 2)
                    probs_T(1, 3)
                    expert_columns(0, 0)
                    pe.wait_ge(pT_done, 2 * DC)
                if b:
                    pe.wait_ge(y_done, s - 1)
                expert_columns(s - 1, 1)
                pe.wait_ge(pT_done, DC * s + 3)
                denominators_T(s)
                attention(s)
                scores(s + 2, 0)
                if b + 2 < B:
                    tokens_T(b + 2, 0)
                scores(s + 2, 1)
                if b + 2 < B:
                    pe.wait_ge(rT_done, s + 1)
                    tokens_T(b + 2, 1)
                scores(s + 2, 2)
                if b + 2 < B:
                    pe.wait_ge(xT_lo_done, TB * (b + 2) + 1)
                gated_T(s - 1)
                out_projection(s)
                expert_output(s - 1)
                if b + 2 < B:
                    pe.wait_ge(xT_lo_done, TB * (b + 3))
                probs_T(s + 1, 0)
                scores(s + 2, 3)

            t = NT - 2
            probs_T(t, 1)
            pe.wait_ge(pT_done, DC * t + 1)
            tokens2_T(t - 1)
            pe.wait_ge(sub_done, SB * NT - 1)
            probs_T(t, 2)
            probs_T(t, 3)
            pe.wait_ge(y_done, t - 1)
            expert_columns(t - 1, 1)
            expert_columns(t - 1, 0)
            pe.wait_ge(pT_done, DC * t + 2)
            denominators_T(t)
            attention(t)
            probs_T(t + 1, 0)
            pe.wait_ge(rT_done, t + 1)
            gated_T(t - 1)
            probs_T(t + 1, 1)
            probs_T(t + 1, 2)
            probs_T(t + 1, 3)
            pe.wait_ge(sub_done, SB * NT)
            out_projection(t)
            pe.wait_ge(pT_done, DC * (t + 1) + 1)
            denominators_T(t + 1)
            attention(t + 1)
            expert_output(t - 1, (0, 1))
            tokens2_T(t)
            expert_output(t - 1, (2,))
            out_projection(t + 1)
            expert_output(t - 1, (3,))
            expert_columns(t, 1)
            expert_columns(t, 0)
            pe.wait_ge(xn2_ready, NT)
            last_halves("x2T", xn2)
            expert_columns(t + 1, 1)
            gated_T(t)
            pe.wait_ge(y_done, t)
            expert_columns(t + 1, 0)
            expert_output(t, (0, 1))
            pe.wait_ge(zg_done, NT)
            last_halves("zgT", zg)
            expert_output(t, (2, 3))
            expert_output(t + 1)


def kernel(**inputs):
    import numpy as _np
    import concourse.bacc as _bacc
    from concourse import mybir as _mybir
    from concourse.bass_utils import run_bass_kernel_spmd as _run

    i = {k: _np.asarray(a) for k, a in inputs.items()}

    def on_partitions(a):
        return a.reshape(a.shape[0] // 128, 128, *a.shape[1:]).swapaxes(0, 1)

    laid = {
        "x": i["x"],
        "ctxT": on_partitions(i["ctx_4096"].transpose(2, 0, 1)),
        "maskT": i["mask_SxS2_bk0"].T,
        "g_attn": i["g_xattn"],
        "g_ffn": i["g_ffn"],
        "wqT": on_partitions(i["L0_xattn_w_q"].T),
        "wkT": on_partitions(i["L0_xattn_w_k"].T),
        "wvT": on_partitions(i["L0_xattn_w_v"].T),
        "woT": on_partitions(i["L0_xattn_w_out"].T),
        "aT": on_partitions(i["L0_ffn_A_w"].T),
        "bT": on_partitions(i["L0_ffn_B_w"].T),
        "wr": i["L0_ffn_Wq_w"],
        "keysT": i["L0_ffn_keys"].T,
    }
    nc = _bacc.Bacc("TRN2", target_bir_lowering=False, num_devices=1)
    arrays, args = {}, []
    for name, a in laid.items():
        a = _np.ascontiguousarray(a)
        arrays[f"in_{name}"] = a
        args.append(nc.dram_tensor(f"in_{name}", a.shape, _mybir.dt.from_np(a.dtype), kind="ExternalInput").ap())
    args.append(nc.dram_tensor("out_x", i["x"].shape, _mybir.dt.float32, kind="ExternalOutput").ap())
    gated_cross_attention_kernel(nc, *args)
    r = _run(nc, [arrays], core_ids=[0])
    return r.results[0]["out_x"]
```
